# Optimizing a Trainium2 kernel written in Bass

```python
import numpy as np
import jax
import jax.numpy as jnp

def _softmax(x, axis=-1):
    return jax.nn.softmax(x, axis=axis)

def _gelu(x):
    return jax.nn.gelu(x, approximate=True)

def _silu(x):
    return jax.nn.silu(x)

def _sigmoid(x):
    return jax.nn.sigmoid(x)

def _layernorm(x, axis=-1, eps=1e-05):
    m = jnp.mean(x, axis=axis, keepdims=True)
    v = jnp.var(x, axis=axis, keepdims=True)
    return (x - m) / jnp.sqrt(v + eps)

def _scatter_add(tgt, idx, src, axis=0):
    return tgt.at[idx].add(src)

def _segment_sum(src, seg, n):
    return jax.ops.segment_sum(src, seg, n)
kernel_name = 'mk_perceiver_d1_seqx_r2_ca53b5'

def setup_inputs(seed: int=0):
    np.random.seed(seed)
    _w = jnp.asarray

    def _rec_inputs():
        import jax
        import jax.numpy as jnp
        _rk = jax.random.key(seed)
        x = 7.22e-05 + 1 * jax.random.normal(jax.random.fold_in(_rk, 1), (8, 64, 512), jnp.float32)
        _lenS = 64 - jax.random.randint(jax.random.fold_in(_rk, 7), (8,), 0, max(1, 64 // 4) + 1, jnp.int32)
        _lenS2 = 1601 - jax.random.randint(jax.random.fold_in(_rk, 8), (8,), 0, max(1, 1601 // 4) + 1, jnp.int32)
        _ctx_1024P = jax.random.normal(jax.random.fold_in(_rk, 11), (8, 16, 512), jnp.float32)
        _ctx_1024c = jax.random.dirichlet(jax.random.fold_in(_rk, 511), 0.3 * jnp.ones((16,), jnp.float32), (8, 1601))
        _ctx_1024t = jnp.einsum('bsk,bkd->bsd', _ctx_1024c, _ctx_1024P)
        _ctx_1024t = _ctx_1024t * jax.lax.rsqrt(jnp.mean(jnp.square(_ctx_1024t)) + 1e-12) * 0.953939
        ctx_1024 = 4.13588e-05 + 0.999923 * (_ctx_1024t + 0.3 * jax.random.normal(jax.random.fold_in(_rk, 611), (8, 1601, 512), jnp.float32))
        _validS = jnp.arange(64)[None, :] < _lenS[:, None]
        _validS2 = jnp.arange(1601)[None, :] < _lenS2[:, None]
        _causal = jnp.tril(jnp.ones((64, 64), dtype=bool))
        mask_BxS2_ik0 = jnp.where(jnp.broadcast_to(_validS2[:, :], (8, 1601)), 0, 1).astype(jnp.int32)
        return (x, ctx_1024, mask_BxS2_ik0)
    x, ctx_1024, mask_BxS2_ik0 = _rec_inputs()

    def _L0_xattn_setup():
        import jax, jax.numpy as jnp
        import numpy as np
        B, LQ, LK, D = (4, 1024, 1024, 512)
        H = 16
        HD = D // H

        def _split_heads(x):
            b, l, _ = x.shape
            return x.reshape(b, l, H, HD).transpose(0, 2, 1, 3)
        key = jax.random.key(seed)
        ks = jax.random.split(key, 10)
        s = 0.02
        return {'hidden_states': jax.random.normal(ks[0], (B, LQ, D), jnp.float32), 'context': jax.random.normal(ks[1], (B, LK, D), jnp.float32), 'attention_mask': jax.random.randint(ks[2], (B, LK), 0, 2, jnp.int32), 'q_w': jax.random.normal(ks[3], (D, D), jnp.float32) * s, 'q_b': jnp.zeros((D,), jnp.float32), 'k_w': jax.random.normal(ks[4], (D, D), jnp.float32) * s, 'k_b': jnp.zeros((D,), jnp.float32), 'v_w': jax.random.normal(ks[5], (D, D), jnp.float32) * s, 'v_b': jnp.zeros((D,), jnp.float32)}
    _L0_xattn_all = _L0_xattn_setup()
    _L0_xattn_in = {k: v for k, v in _L0_xattn_all.items() if k in ('q_w', 'q_b', 'k_w', 'k_b', 'v_w', 'v_b')}
    del _L0_xattn_all

    def _L0_attn_setup():
        import jax, jax.numpy as jnp
        import numpy as np
        import math
        HIDDEN = 512
        NUM_LAYERS = 24
        INIT_RANGE = 0.02
        key = jax.random.key(seed)
        k1, k2 = jax.random.split(key)
        B, S, H = (4, 2048, HIDDEN)
        hidden_states = jax.random.normal(k1, (B, S, H), dtype=jnp.float32)
        std = INIT_RANGE / math.sqrt(2.0 * NUM_LAYERS * H)
        W_q = jax.random.normal(k2, (H, H), dtype=jnp.float32) * std
        return {'hidden_states': hidden_states, 'W_q': W_q}
    _L0_attn_all = _L0_attn_setup()
    _L0_attn_in = {k: v for k, v in _L0_attn_all.items() if k in ('W_q',)}
    del _L0_attn_all

    def _L0_ffn_setup():
        import jax, jax.numpy as jnp
        import numpy as np
        D_MODEL = 512
        D_FF = 2048
        NUM_EXPERTS = 8
        TOP_K = 2
        B, S = (4, 512)
        key = jax.random.key(seed)
        ks = jax.random.split(key, 8)
        scale_in = 1.0 / np.sqrt(D_MODEL)
        scale_ff = 1.0 / np.sqrt(D_FF)
        return {'x': jax.random.normal(ks[0], (B, S, D_MODEL), dtype=jnp.float32), 'gate_w': jax.random.normal(ks[1], (D_MODEL, NUM_EXPERTS), dtype=jnp.float32) * scale_in, 'gate_b': jnp.zeros((NUM_EXPERTS,), dtype=jnp.float32), 'w1': jax.random.normal(ks[2], (NUM_EXPERTS, D_MODEL, D_FF), dtype=jnp.float32) * scale_in, 'b1': jnp.zeros((NUM_EXPERTS, D_FF), dtype=jnp.float32), 'w2': jax.random.normal(ks[3], (NUM_EXPERTS, D_FF, D_MODEL), dtype=jnp.float32) * scale_ff, 'b2': jnp.zeros((NUM_EXPERTS, D_MODEL), dtype=jnp.float32)}
    _L0_ffn_all = _L0_ffn_setup()
    _L0_ffn_in = {k: v for k, v in _L0_ffn_all.items() if k in ('gate_w', 'gate_b', 'w1', 'b1', 'w2', 'b2')}
    del _L0_ffn_all
    return {'x': x, 'ctx_1024': ctx_1024, 'mask_BxS2_ik0': mask_BxS2_ik0, 'L0_xattn_q_w': _L0_xattn_in['q_w'], 'L0_xattn_q_b': _L0_xattn_in['q_b'], 'L0_xattn_k_w': _L0_xattn_in['k_w'], 'L0_xattn_k_b': _L0_xattn_in['k_b'], 'L0_xattn_v_w': _L0_xattn_in['v_w'], 'L0_xattn_v_b': _L0_xattn_in['v_b'], 'L0_attn_W_q': _L0_attn_in['W_q'], 'L0_ffn_gate_w': _L0_ffn_in['gate_w'], 'L0_ffn_gate_b': _L0_ffn_in['gate_b'], 'L0_ffn_w1': _L0_ffn_in['w1'], 'L0_ffn_b1': _L0_ffn_in['b1'], 'L0_ffn_w2': _L0_ffn_in['w2'], 'L0_ffn_b2': _L0_ffn_in['b2']}

def reference(x, ctx_1024, mask_BxS2_ik0, L0_xattn_q_w, L0_xattn_q_b, L0_xattn_k_w, L0_xattn_k_b, L0_xattn_v_w, L0_xattn_v_b, L0_attn_W_q, L0_ffn_gate_w, L0_ffn_gate_b, L0_ffn_w1, L0_ffn_b1, L0_ffn_w2, L0_ffn_b2):
    import jax
    import jax.numpy as jnp

    def _L0_xattn_ref(hidden_states, context, attention_mask, q_w, q_b, k_w, k_b, v_w, v_b):
        import jax, jax.numpy as jnp
        import numpy as np
        B, LQ, LK, D = (4, 1024, 1024, 512)
        H = 16
        HD = D // H

        def _split_heads(x):
            b, l, _ = x.shape
            return x.reshape(b, l, H, HD).transpose(0, 2, 1, 3)
        q = _split_heads(hidden_states @ q_w.T + q_b)
        k = _split_heads(context @ k_w.T + k_b)
        v = _split_heads(context @ v_w.T + v_b)
        scores = jnp.einsum('bhqd,bhkd->bhqk', q, k) / jnp.sqrt(jnp.float32(HD))
        mask = (attention_mask > 0)[:, None, None, :]
        scores = jnp.where(mask, -jnp.inf, scores)
        probs = jax.nn.softmax(scores, axis=-1)
        ctx = jnp.einsum('bhqk,bhkd->bhqd', probs, v)
        ctx = ctx.transpose(0, 2, 1, 3).reshape(ctx.shape[0], ctx.shape[2], H * HD)
        return ctx

    def _L0_attn_ref(hidden_states, W_q):
        import jax, jax.numpy as jnp
        import numpy as np
        import math
        HIDDEN = 512
        NUM_LAYERS = 24
        INIT_RANGE = 0.02
        q = jnp.einsum('bsh,oh->bso', hidden_states, W_q)
        pre_attn = jnp.einsum('bso,bto->bst', q, hidden_states)
        attention = jnp.einsum('bst,bth->bsh', pre_attn, hidden_states)
        return attention

    def _L0_ffn_ref(x, gate_w, gate_b, w1, b1, w2, b2):
        import jax, jax.numpy as jnp
        import numpy as np
        D_MODEL = 512
        D_FF = 2048
        NUM_EXPERTS = 8
        TOP_K = 2
        B, S = (4, 512)
        b, s, d = x.shape
        xf = x.reshape(-1, d)
        T = xf.shape[0]
        logits = xf @ gate_w + gate_b
        top_v, top_i = jax.lax.top_k(logits, TOP_K)
        top_w = jax.nn.softmax(top_v, axis=-1)
        cw = jnp.zeros((T, NUM_EXPERTS), dtype=x.dtype)
        cw = cw.at[jnp.arange(T)[:, None], top_i].add(top_w)
        out = jnp.zeros_like(xf)
        for e in range(NUM_EXPERTS):
            h = jax.nn.relu(xf @ w1[e] + b1[e])
            y = h @ w2[e] + b2[e]
            out = out + cw[:, e:e + 1] * y
        return out.reshape(b, s, d)
    x = x + _L0_xattn_ref(_layernorm(x, axis=-1), ctx_1024, mask_BxS2_ik0, L0_xattn_q_w, L0_xattn_q_b, L0_xattn_k_w, L0_xattn_k_b, L0_xattn_v_w, L0_xattn_v_b)
    x = x + _L0_attn_ref(_layernorm(x, axis=-1), L0_attn_W_q)
    x = x + _L0_ffn_ref(_layernorm(x, axis=-1), L0_ffn_gate_w, L0_ffn_gate_b, L0_ffn_w1, L0_ffn_b1, L0_ffn_w2, L0_ffn_b2)
    return x

_drawn_inputs = setup_inputs


def setup_inputs(seed=0):
    import zlib

    import numpy as np

    out = dict(_drawn_inputs(seed))
    spreads = {'L0_xattn_q_b': (0.0, 0.289),
     'L0_xattn_k_b': (0.0, 0.8),
     'L0_xattn_v_b': (0.0, 0.1),
     'L0_ffn_gate_b': (0.0, 0.1),
     'L0_ffn_b1': (0.0, 0.1),
     'L0_ffn_b2': (0.0, 0.1)}
    factors = {}
    for name, (base, spread) in spreads.items():
        noise = np.random.default_rng([zlib.crc32(name.encode()), seed]).standard_normal(out[name].shape)
        drawn = base * np.exp(spread * noise) if base else spread * noise
        out[name] = jnp.asarray(drawn.astype(out[name].dtype))
    for name, factor in factors.items():
        out[name] = (out[name] * factor).astype(out[name].dtype)
    return out
```

```python
from contextlib import ExitStack

import concourse.bass as bass
from concourse import mybir

ALU = mybir.AluOpType
ACT = mybir.ActivationFunctionType
AX = mybir.AxisListType
F32 = mybir.dt.float32
F32R = mybir.dt.float32r
BF16 = mybir.dt.bfloat16
I32 = mybir.dt.int32
U32 = mybir.dt.uint32

P = 128
BANK = 512
B, S, D = 8, 64, 512
T = B * S
TT = T // P
C = D // P
LK = 1601
HD = 32
HPC = P // HD
KT = -(-LK // P)
KP = KT * P
KC = 402
NKC = 4
LKP = KC * NKC
CC = KP // NKC
E, F = 8, 2048
NP = F // 512
FC = 4
SCALE = float(HD) ** -0.5
EPS = 1e-5
LOWEST = -3.0e38


def steps_of(last):
    steps = []
    for h in range(2):
        v = [("v", h, j) for j in range((KT + 1) // 2)]
        k = [] if h and last else [("k", 1 - h, j) for j in range(2 * NKC)]
        steps += v[:3]
        for r in range(4):
            steps += [("s", 4 * h + r, j) for j in range(NKC)] + v[3 + r:4 + r]
        steps += k[:6] + [("r", 2 * h, 0), ("r", 2 * h + 1, 0)] + k[6:7]
        steps += [("w", 2 * h, 0)] + k[7:] + [("w", 2 * h + 1, 0)]
    return steps


STEPS = [steps_of(False), steps_of(True)]
ITEMS = [[s for s in steps if s[0] != "w"] for steps in STEPS]
KV = [[s for s in items if s[0] in "kv"] for items in ITEMS]
NW = len(ITEMS[0])
NKV = len(KV[0])
FIRST_K = 2 * NKC
NPT = 2 * (KT + 1)
PTD = 3
TPH = KT // 2 + 1


def count(b, last, step):
    return NW * b + FIRST_K + ITEMS[last].index(step) + 1


def before_bank(b, i):
    return NW * b + FIRST_K + (i - 3 if i >= 4 else (-1, 0, -1, 0)[i])


def pt_before(j):
    last = j - PTD if j >= PTD else max(m for m in range(NPT) if m % PTD == j) - NPT
    return last + 1 + PTD


def layer(nc, x, ctxT, mask, qwT, kwT, vwT, wqT, bias3, gate_w, gate_b, w1, b1, w2, b2, out):
    with ExitStack() as top:
        def sem(name):
            return top.enter_context(nc.semaphore(name))

        def sb(stack, name, shape, dt):
            return stack.enter_context(nc.sbuf_tensor(name, shape, dt))

        work = [top.enter_context(nc.psum_tensor(f"work{i}", [P, BANK], F32)) for i in range(4)]
        ptp = [top.enter_context(nc.psum_tensor(f"ptp{i}", [P, BANK], F32)) for i in range(3)]
        pv = top.enter_context(nc.psum_tensor("pv", [P, BANK], F32))

        ident = sb(top, "ident", [P, P], F32)
        ones = sb(top, "ones", [P, P], F32)
        qT = sb(top, "qT", [P, C, T], F32)
        biasT = sb(top, "biasT", [P, 3 * C], F32)
        stat = sb(top, "stat", [P, 64], F32)

        with ExitStack() as m:
            kw = [sb(m, f"kw_{n}", [P, C, D], F32R) for n in ("hi", "lo")]
            vw = [sb(m, f"vw_{n}", [P, C, D], F32R) for n in ("hi", "lo")]
            cx = [sb(m, f"cx_{n}", [P, C, KP], F32R) for n in ("hi", "lo")]
            kk = [sb(m, f"kk_{n}", [P, 2, LKP], F32R) for n in ("hi", "lo")]
            pr = sb(m, "pr", [P, 4, KP], F32)
            negmask = sb(m, "negmask", [P, LKP], BF16)
            raw = sb(m, "raw", [P, 2, C, CC], F32)
            qbd = [sb(m, f"qbd_{n}", [P, 2, 2, P], F32R) for n in ("hi", "lo")]
            diag = sb(m, "diag", [P, 4, P], F32)
            recip = sb(m, "recip", [P, 2, 2 * P], F32)
            smx = sb(m, "smx", [P, 8, NKC], F32)
            nmx = sb(m, "nmx", [P, 8], F32)
            rsum = sb(m, "rsum", [P, 8], F32)
            rinv = sb(m, "rinv", [P, 8], F32)
            with ExitStack() as m2:
                vv = [sb(m2, f"vv_{n}", [P, KT, 2 * P], F32R) for n in ("hi", "lo")]
                pt = [sb(m2, f"pt_{n}", [P, PTD, 2, 2 * P], F32R) for n in ("hi", "lo")]
            xin = sb(m, "xin", [P, TT, D], F32)
            xnT = sb(m, "xnT", [P, C, T], F32)
            wraw = sb(m, "wraw", [P, C, D], F32)
            brow = sb(m, "brow", [3 * C, P], F32)

        with ExitStack() as m:
            xs = sb(m, "xs", [P, TT, D], F32)
            hn = sb(m, "hn", [P, TT, D], F32)
            hT = sb(m, "hT", [P, C, T], F32)
            gw = sb(m, "gw", [P, C, E], F32)
            gb = sb(m, "gb", [P, E], F32)
            b1r = sb(m, "b1r", [P, P], F32)
            b1T = sb(m, "b1T", [P, P], F32)
            b2s = sb(m, "b2s", [E, D], F32)
            logit = sb(m, "logit", [P, TT, E], F32)
            top8 = sb(m, "top8", [P, TT, 8], F32)
            idx8 = sb(m, "idx8", [P, TT, 8], U32)
            idxf = sb(m, "idxf", [P, TT, 8], F32)
            iota_e = sb(m, "iota_e", [P, E], F32)
            wts = sb(m, "wts", [P, 4, TT], F32)
            cw = sb(m, "cw", [P, TT, E], F32)
            cw2 = sb(m, "cw2", [P, TT, E], F32)
            cwT = sb(m, "cwT", [E, T], F32)
            pre = sb(m, "pre", [P, TT, P], F32)
            xT = [sb(m, f"xT_{n}", [P, C, T], F32R) for n in ("hi", "lo")]
            w1raw = sb(m, "w1raw", [P, 2, C, 512], F32)
            w2raw = sb(m, "w2raw", [P, 2, FC, D], F32)
            w1s = [sb(m, f"w1_{n}", [P, 2, C, 512], F32R) for n in ("hi", "lo")]
            hf = sb(m, "hf", [P, 2, T], F32)
            hs = [sb(m, f"h_{n}", [P, 2, FC, T], F32R) for n in ("hi", "lo")]
            with ExitStack() as m2:
                w2s = [sb(m2, f"w2_{n}", [P, 2, FC, D], F32R) for n in ("hi", "lo")]
            wq2 = sb(m, "wq2", [P, C, D], F32)
            gT = sb(m, "gT", [P, C, T], F32)

        ld_x, ld_b, ld_w = sem("x_loaded"), sem("biases_loaded"), [sem(f"weight{i}_loaded") for i in range(3)]
        ld_raw = [sem(f"context_chunk_loaded{i}") for i in range(2)]
        ld_mask = sem("mask_loaded")
        consts = sem("constants_ready")
        chain = sem("vector_step")
        ln1 = sem("x_normalised")
        var_done, root_done = sem("variance_ready"), sem("root_ready")
        t_full = sem("pre_psum_full")
        t_out = sem("pre_psum_drained")
        w_hi, w_lo = sem("weight_hi"), sem("weight_lo")
        c_hi, c_lo = sem("context_hi"), sem("context_lo")
        q_done = sem("queries_ready")
        qbd_done = sem("query_blocks_ready")
        w_full = sem("work_bank_full")
        kv_hi = sem("keys_values_hi")
        w_free = sem("work_bank_drained")
        raw_nmx = sem("raw_row_maximum")
        nmx_done = sem("row_maximum_ready")
        exp_done = sem("row_exponentials_ready")
        rinv_done = sem("row_reciprocal")
        diag_done = sem("reciprocal_diagonal_ready")
        pt_full, pt_hi, pt_lo = sem("probabilities_transposed"), sem("probabilities_hi"), sem("probabilities_lo")
        pt_used = sem("probabilities_used")
        pv_free = sem("weighted_values_drained")
        mask_done = sem("mask_ready")
        att_over = sem("attention_over")
        ld2 = [sem(f"late_load{i}") for i in range(6)]
        zeroed = sem("late_constants_ready")
        ob_done = sem("attention_bias_added")
        m_full, m_out = sem("mid_psum_full"), sem("mid_psum_copied")
        x_add, ln2 = sem("residual_added"), sem("residual_normalised")
        pre_done = sem("self_scores_ready")
        gate_diff, gate_exp = sem("gate_difference"), sem("gate_exponential")
        x_hi, x_lo = sem("moe_input_hi"), sem("moe_input_lo")
        cw_done, cwT_done = sem("expert_weights_ready"), sem("expert_weights_transposed")
        ld_w1 = [sem(f"w1_loaded{i}") for i in range(2)]
        ld_w2 = [sem(f"w2_loaded{i}") for i in range(2)]
        w1_hi, w1_lo, w2_hi, w2_lo = sem("w1_hi"), sem("w1_lo"), sem("w2_hi"), sem("w2_lo")
        h_full, h_relu, h_hi, h_lo = sem("hidden_full"), sem("hidden_relu"), sem("hidden_hi"), sem("hidden_lo")
        p2_used = sem("w2_piece_used")
        y_out = sem("expert_output_added")
        stored = sem("output_stored")

        LASTB, LASTE = B - 1, E - 1
        yb = ptp + [pv]
        block = top.enter_context(nc.Block())

        def own(eng, sem, value):
            eng.wait_ge(sem, value)
            if not isinstance(value, int):
                eng.nop(nofuse=True)

        @block.sync
        def _(sp):
            sp.dma_start(xin[:], x.rearrange("(t p) d -> p t d", p=P)).then_inc(ld_x, 16)
            sp.dma_start(brow[:], bias3).then_inc(ld_b, 16)
            sp.dma_start(wraw[:], qwT.rearrange("(c p) n -> p c n", p=P)).then_inc(ld_w[0], 16)

            def load_chunk(b, k, first=False):
                if not first:
                    own(sp, c_lo, NKC * b + k - 1)
                src = ctxT[b:b + 1] if isinstance(b, int) else ctxT[bass.ds(b, 1)]
                sp.dma_start(raw[:, k % 2], src[:, :, k * CC:(k + 1) * CC].rearrange(
                    "o (c p) n -> p (o c) n", p=P)).then_inc(ld_raw[k % 2], 16)

            def load_mask(b):
                src = mask[b:b + 1, :] if isinstance(b, int) else mask[bass.ds(b, 1), :]
                sp.dma_start(pr[:, 0, 0:LK].bitcast(I32), src.broadcast_to([P, LK])).then_inc(ld_mask, 16)

            load_chunk(0, 0, True)
            load_chunk(0, 1, True)
            load_mask(0)
            sp.wait_ge(t_full, 2 * C + 1)
            sp.dma_start(wraw[:], kwT.rearrange("(c p) n -> p c n", p=P)).then_inc(ld_w[1], 16)
            sp.wait_ge(w_lo, 1)
            sp.dma_start(wraw[:], vwT.rearrange("(c p) n -> p c n", p=P)).then_inc(ld_w[2], 16)
            load_chunk(0, 2)
            load_chunk(0, 3)

            with sp.Fori(0, LASTB) as b:
                for k in range(NKC):
                    load_chunk(b + 1, k)
                own(sp, pt_full, NPT * b + 3 * TPH)
                load_mask(b + 1)

            sp.wait_ge(att_over, 4)
            sp.dma_start(xs[:], x.rearrange("(t p) d -> p t d", p=P)).then_inc(ld2[0], 16)
            sp.dma_start(b1r[:], b1.rearrange("e (k j) -> (e k) j", j=P)).then_inc(ld2[4], 16)
            sp.dma_start(wq2[:], wqT.rearrange("(c p) n -> p c n", p=P)).then_inc(ld2[1], 16)
            sp.dma_start(gw[:], gate_w.rearrange("(c p) n -> p c n", p=P)).then_inc(ld2[2], 16)
            sp.dma_start(gb[:], gate_b.broadcast_to([P, E])).then_inc(ld2[3], 16)
            sp.dma_start(b2s[:], b2).then_inc(ld2[5], 16)

            def load_w1(e, p, first=False):
                s = p % 2
                if not first:
                    own(sp, w1_lo, NP * e + p - 1)
                src = w1[e:e + 1] if isinstance(e, int) else w1[bass.ds(e, 1)]
                sp.dma_start(w1raw[:, s], src[:, :, p * 512:(p + 1) * 512].rearrange(
                    "o (c p) n -> p (o c) n", p=P)).then_inc(ld_w1[s], 16)

            def load_w2(e, p, first=False):
                s = p % 2
                if not first:
                    own(sp, w2_lo, NP * e + p - 1)
                src = w2[e:e + 1] if isinstance(e, int) else w2[bass.ds(e, 1)]
                sp.dma_start(w2raw[:, s], src[:, p * 512:(p + 1) * 512, :].rearrange(
                    "o (c p) n -> p (o c) n", p=P)).then_inc(ld_w2[s], 16)

            load_w1(0, 0, True)
            load_w1(0, 1, True)
            load_w2(0, 0, True)
            load_w1(0, 2)
            load_w2(0, 1, True)
            load_w1(0, 3)
            load_w2(0, 2)
            load_w1(1, 0)
            load_w2(0, 3)

            def expert(e, last=False):
                for p in range(NP):
                    if p < NP - 1:
                        load_w1(e, p + 1)
                    elif not last:
                        load_w1(e + 1, 0)
                    load_w2(e, p)

            with sp.Fori(1, LASTE) as e:
                expert(e)
            expert(LASTE, True)
            sp.wait_ge(y_out, TT * (E + 1))
            sp.dma_start(out.rearrange("(t p) d -> p t d", p=P), xs[:]).then_inc(stored, 16)
            sp.wait_ge(stored, 16)

        @block.gpsimd
        def _(pool):
            pool.memset(ident[:], 0.0).then_inc(consts, 1)
            pool.memset(ones[:], 1.0).then_inc(consts, 1)
            pool.wait_ge(consts, 2)
            pool.affine_select(out=ident[:], in_=ident[:], compare_op=ALU.not_equal, fill=1.0, base=0,
                               pattern=[[-1, P]], channel_multiplier=1).then_inc(consts, 1)
            for q in qbd:
                pool.memset(q[:].bitcast(F32), 0.0).then_inc(consts, 1)
            pool.memset(pr[:, :, LKP:KP], 0.0).then_inc(consts, 1)
            pool.wait_ge(consts, 6)

            def ctx_lo(b, k):
                own(pool, c_hi, NKC * b + k + 1)
                sl = slice(k * CC, (k + 1) * CC)
                pool.tensor_tensor(cx[1][:, :, sl], raw[:, k % 2], cx[0][:, :, sl].bitcast(F32),
                                   ALU.subtract).then_inc(c_lo, 1)

            for k in range(NKC):
                ctx_lo(0, k)
            with pool.Fori(1, B) as b:
                for k in range(NKC):
                    ctx_lo(b, k)
            pool.wait_ge(c_lo, NKC * B)
            pool.sem_inc(att_over, 1)

            pool.wait_ge(att_over, 4)
            pool.iota(iota_e[:], pattern=[[1, E]], base=0, channel_multiplier=0,
                      allow_small_or_imprecise_dtypes=True).then_inc(zeroed, 1)
            pool.memset(pre[:], 0.0).then_inc(zeroed, 1)

            def expert(e, first=False):
                for p in range(NP):
                    if not (first and p < 2):
                        own(pool, p2_used, NP * e + p - 1)
                    for f in range(FC):
                        own(pool, h_relu, FC * (NP * e + p) + f + 1)
                        pool.tensor_copy(hs[0][:, p % 2, f], hf[:, f % 2]).then_inc(h_hi, 1)

            expert(0, True)
            with pool.Fori(1, E) as e:
                expert(e)

        @block.scalar
        def _(act):
            def copy(dst, src, signal):
                act.activation(dst, src, ACT.Copy).then_inc(signal, 1)

            def ctx_hi(b, k):
                act.wait_ge(ld_raw[k % 2], 16 * (2 * b + k // 2 + 1))
                copy(cx[0][:, :, k * CC:(k + 1) * CC], raw[:, k % 2], c_hi)

            def root(o):
                act.wait_ge(var_done, o)
                act.activation(stat[:, 44:48], stat[:, 40:44], ACT.Sqrt).then_inc(root_done, 1)

            root(1)
            ctx_hi(0, 0)
            ctx_hi(0, 1)
            for c in range(C):
                act.wait_ge(t_full, c + 1)
                copy(xnT[:, c], work[c][:], t_out)
            act.wait_ge(t_full, C + 1)
            copy(biasT[:], pv[:, 0:3 * C], t_out)
            act.wait_ge(t_out, C + 1)
            for c in range(C):
                act.wait_ge(t_full, C + 2 + c)
                act.activation(qT[:, c], work[c][:], ACT.Identity, bias=biasT[:, c:c + 1]).then_inc(q_done, 1)
            for i, w in enumerate((kw, vw)):
                act.wait_ge(ld_w[1 + i], 16)
                copy(w[0][:], wraw[:], w_hi)
            ctx_hi(0, 2)
            ctx_hi(0, 3)

            def key_hi(h, j, bank):
                k, m = j // 2, j % 2
                act.activation(kk[0][:, m, k * KC:(k + 1) * KC], work[bank][:, 0:KC], ACT.Identity,
                               bias=biasT[:, C + 2 * h + m:C + 2 * h + m + 1]).then_inc(kv_hi, 1)

            def kv_item(b, last, step):
                kind, h, j = step
                bank = ITEMS[last].index(step) % 4
                act.wait_ge(w_full, count(b, last, step))
                if kind == "k":
                    key_hi(h, j, bank)
                else:
                    n = min(2, KT - 2 * j)
                    copy(vv[0][:, 2 * j:2 * j + n, :],
                         work[bank][:, 0:n * 2 * P].rearrange("p (n d) -> p n d", n=n), kv_hi)

            for j in range(FIRST_K):
                act.wait_ge(w_full, j + 1)
                key_hi(0, j, j % 4)

            def exponentials(b, r):
                act.wait_ge(nmx_done, 8 * b + r + 1)
                row = pr[:, r % 4, 0:LKP]
                act.activation(row, row, ACT.Exp, bias=nmx[:, r:r + 1],
                               accum_out=rsum[:, r:r + 1]).then_inc(exp_done, 1)

            def pt_item(b, j):
                act.wait_ge(pt_full, NPT * b + j + 1)
                act.wait_ge(pt_used, NPT * b + pt_before(j))
                n = min(2, KT - 2 * (j % TPH))
                copy(pt[0][:, j % PTD, 0:n], ptp[j % PTD][:, 0:n * 2 * P].rearrange("p (n d) -> p n d", n=n), pt_hi)

            LAST_READ = {(CC * (k + 1) - 1) // (2 * P): k for k in range(NKC)}

            def body(b, last=False):
                for step in STEPS[last]:
                    kind, a, j = step
                    if kind in "kv":
                        kv_item(b, last, step)
                    if kind == "v" and a == 1 and j in LAST_READ and not last:
                        ctx_hi(b + 1, LAST_READ[j])
                    if kind == "v" and j >= 3:
                        exponentials(b, 4 * a + j - 3)
                    if kind == "w":
                        lo, hi = (0, TPH + 2) if a % 2 == 0 else (TPH + 2, 2 * TPH)
                        for i in range(lo, hi):
                            pt_item(b, 2 * TPH * (a // 2) + i)

            with act.Fori(0, LASTB) as b:
                body(b)
            body(LASTB, True)
            act.wait_ge(pt_hi, NPT * B)
            act.sem_inc(att_over, 1)

            act.wait_ge(att_over, 4)
            for c in range(C):
                act.activation(qT[:, c], qT[:, c], ACT.Identity,
                               bias=biasT[:, 2 * C + c:2 * C + c + 1]).then_inc(ob_done, 1)
            act.wait_ge(m_full, 5)
            copy(b1T[:], pv[:, 0:P], m_out)
            root(2)
            for t in range(TT):
                act.wait_ge(m_full, 6 + t)
                copy(hT[:, :, t * P:(t + 1) * P], yb[t][:].rearrange("p (c n) -> p c n", c=C), m_out)
            for c in range(C):
                act.wait_ge(m_full, 10 + c)
                copy(gT[:, c], work[c][:], m_out)
            root(3)
            for t in range(TT):
                act.wait_ge(m_full, 22 + t)
                copy(hT[:, :, t * P:(t + 1) * P], yb[t][:].rearrange("p (c n) -> p c n", c=C), m_out)
                copy(xT[0][:, :, t * P:(t + 1) * P], yb[t][:].rearrange("p (c n) -> p c n", c=C), x_hi)
            act.wait_ge(gate_diff, 1)
            act.activation(wts[:, 1], wts[:, 0], ACT.Exp).then_inc(gate_exp, 1)

            def w1_part(e, p, first=False):
                s = p % 2
                act.wait_ge(ld_w1[s], 16 * (2 * e + p // 2 + 1))
                if not first:
                    act.wait_ge(h_full, FC * (NP * e + p - 1))
                copy(w1s[0][:, s], w1raw[:, s], w1_hi)

            def w2_part(e, p, first=False):
                s = p % 2
                act.wait_ge(ld_w2[s], 16 * (2 * e + p // 2 + 1))
                if not first:
                    act.wait_ge(p2_used, NP * e + p - 1)
                copy(w2s[0][:, s], w2raw[:, s], w2_hi)

            def expert(e, first=False, last=False):
                for p in range(NP):
                    if p < NP - 1:
                        w1_part(e, p + 1, first and p == 0)
                    elif not last:
                        w1_part(e + 1, 0)
                    w2_part(e, p, first and p < 2)
                    for f in range(FC):
                        n = FC * (NP * e + p) + f
                        act.wait_ge(h_full, n + 1)
                        if not (first and p == 0 and f < 2):
                            act.wait_ge(h_lo, n - 1)
                        col = 16 * e + FC * p + f
                        bias = b1T[:, col:col + 1] if isinstance(e, int) else b1T[:, bass.ds(col, 1)]
                        act.activation(hf[:, f % 2], work[f][:], ACT.Relu, bias=bias).then_inc(h_relu, 1)

            w1_part(0, 0, True)
            expert(0, first=True)
            with act.Fori(1, LASTE) as e:
                expert(e)
            expert(LASTE, last=True)

        @block.tensor
        def _(pe):
            PASSES = ((0, 0), (0, 1), (1, 0))

            def products(dst, lhs, rhs, n=C):
                for c in range(n):
                    for i, j in PASSES:
                        last = pe.matmul(dst, lhs(i, c), rhs(j, c), start=(c == 0 and (i, j) == (0, 0)),
                                         stop=(c == n - 1 and (i, j) == (1, 0)))
                return last

            def plain(dst, lhs, rhs, n=C):
                for c in range(n):
                    last = pe.matmul(dst, lhs(c), rhs(c), start=(c == 0), stop=(c == n - 1))
                return last

            pe.wait_ge(consts, 3)
            pe.wait_ge(ln1, TT)
            for c in range(C):
                for t in range(TT):
                    last = pe.transpose(work[c][:, t * P:(t + 1) * P], xin[:, t, c * P:(c + 1) * P], ident[:])
                last.then_inc(t_full, 1)
            pe.wait_ge(ld_b, 16)
            pe.transpose(pv[:, 0:3 * C], brow[:], ident[0:3 * C, 0:3 * C]).then_inc(t_full, 1)
            pe.wait_ge(t_out, C + 1)
            pe.wait_ge(ld_w[0], 16)
            for m_ in range(C):
                plain(work[m_][:], lambda c: wraw[:, c, m_ * P:(m_ + 1) * P],
                      lambda c: xnT[:, c]).then_inc(t_full, 1)

            def key_item(b, h, j, bank):
                k, m = j // 2, j % 2
                if m == 0:
                    pe.wait_ge(c_lo, NKC * b + k + 1)
                products(work[bank][:, 0:KC], lambda i, c: kw[i][:, c, (2 * h + m) * P:(2 * h + m + 1) * P],
                         lambda i, c: cx[i][:, c, k * KC:(k + 1) * KC]).then_inc(w_full, 1)

            def value_item(h, j, bank):
                for n in range(min(2, KT - 2 * j)):
                    kt = 2 * j + n
                    last = products(work[bank][:, n * 2 * P:(n + 1) * 2 * P],
                                    lambda i, c: cx[i][:, c, kt * P:(kt + 1) * P],
                                    lambda i, c: vw[i][:, c, h * 2 * P:(h + 1) * 2 * P])
                last.then_inc(w_full, 1)

            def item(b, last, step):
                kind, a, k = step
                i = ITEMS[last].index(step)
                bank = work[i % 4]
                pe.wait_ge(w_free, before_bank(b, i))
                if kind == "k":
                    key_item(b + 1 if a == 0 else b, a, k, i % 4)
                elif kind == "v":
                    value_item(a, k, i % 4)
                elif kind == "s":
                    cc, rt = (a % 4) // 2, a % 2
                    if a % 4 == 0 and k == 0:
                        pe.wait_ge(qbd_done, (2 * b + a // 4 + 1) * 2 * HPC)
                    products(bank[:, 0:KC], lambda i_, c: qbd[i_][:, cc, rt, :],
                             lambda i_, c: kk[i_][:, cc, k * KC:(k + 1) * KC], 1).then_inc(w_full, 1)
                else:
                    pe.wait_ge(diag_done, 8 * b + 2 * a + 2)
                    for rt in range(2):
                        last_mm = pe.matmul(bank[:, rt * P:(rt + 1) * P], ones[:],
                                            diag[:, 2 * (a % 2) + rt], start=True, stop=True)
                    last_mm.then_inc(w_full, 1)

            pe.wait_ge(q_done, C)
            pe.wait_ge(w_lo, 1)
            for j in range(FIRST_K):
                if j >= 4:
                    pe.wait_ge(w_free, j - 3)
                key_item(0, 0, j, j % 4)
            pe.wait_ge(w_lo, 2)
            pe.sem_inc(pt_used, PTD)

            def turn(b, j):
                g, first = j // TPH, 2 * (j % TPH)
                pe.wait_ge(pt_lo, NPT * b + pt_before(j))
                if j % TPH == 0:
                    pe.wait_ge(exp_done, 8 * b + 2 * g + 2)
                for n in range(min(2, KT - first)):
                    for rt in range(2):
                        last = pe.transpose(ptp[j % PTD][:, (2 * n + rt) * P:(2 * n + rt + 1) * P],
                                            pr[:, (2 * g + rt) % 4, (first + n) * P:(first + n + 1) * P], ident[:])
                last.then_inc(pt_full, 1)

            def weigh(b, j):
                g, first = j // TPH, 2 * (j % TPH)
                pe.wait_ge(pt_lo, NPT * b + j + 1 + PTD)
                if first == 0:
                    pe.wait_ge(pv_free, 4 * b + g + 1)
                for n in range(min(2, KT - first)):
                    kt = first + n
                    for i, k in PASSES:
                        last = pe.matmul(pv[:, 0:2 * P], vv[i][:, kt, (g % 2) * P:(g % 2 + 1) * P],
                                         pt[k][:, j % PTD, n], start=(kt == 0 and (i, k) == (0, 0)),
                                         stop=(kt == KT - 1 and (i, k) == (1, 0)))
                last.then_inc(pt_used, 1)

            def weighted(b, last, g):
                first, end = 2 * TPH * (g // 2), 2 * TPH * (g // 2 + 1)
                if g % 2 == 0:
                    pe.wait_ge(w_free, count(b, last, ("v", g // 2, TPH - 1)))
                    turn(b, first)
                    turn(b, first + 1)
                for j in range(TPH * g, TPH * (g + 1)):
                    if j + 2 < end:
                        turn(b, j + 2)
                    weigh(b, j)

            def body(b, last=False):
                for step in STEPS[last]:
                    if step[0] == "w":
                        weighted(b, last, step[1])
                    else:
                        item(b, last, step)

            with pe.Fori(0, LASTB) as b:
                body(b)
            body(LASTB, True)
            pe.sem_inc(att_over, 1)

            pe.wait_ge(ob_done, C)
            for t in range(TT):
                for c in range(C):
                    last = pe.transpose(work[t][:, c * P:(c + 1) * P], qT[:, c, t * P:(t + 1) * P], ident[:])
                last.then_inc(m_full, 1)
            pe.wait_ge(ld2[4], 16)
            pe.transpose(pv[:, 0:P], b1r[:], ident[:]).then_inc(m_full, 1)

            def turn_tiles(k):
                for t in range(TT):
                    pe.wait_ge(ln2, k * TT + t + 1)
                    for c in range(C):
                        last = pe.transpose(yb[t][:, c * P:(c + 1) * P], hn[:, t, c * P:(c + 1) * P], ident[:])
                    last.then_inc(m_full, 1)

            pe.wait_ge(m_out, 1)
            turn_tiles(0)
            pe.wait_ge(m_out, 1 + TT)
            pe.wait_ge(ld2[1], 16)
            for m_ in range(C):
                plain(work[m_][:], lambda c: wq2[:, c, m_ * P:(m_ + 1) * P],
                      lambda c: hT[:, c]).then_inc(m_full, 1)
            pe.wait_ge(m_out, 1 + TT + C)
            for t in range(TT):
                plain(yb[t][:, 0:P], lambda c: hT[:, c, t * P:(t + 1) * P],
                      lambda c: gT[:, c, t * P:(t + 1) * P]).then_inc(m_full, 1)
            for t in range(TT):
                pe.wait_ge(pre_done, 2 * (t + 1))
                pe.matmul(work[t][:], pre[:, t], hn[:, t], start=True, stop=True).then_inc(m_full, 1)
            turn_tiles(1)
            pe.wait_ge(ld2[2], 16)
            for t in range(TT):
                pe.wait_ge(m_out, 1 + TT + C + t + 1)
                plain(work[t][:, 0:E], lambda c: hT[:, c, t * P:(t + 1) * P],
                      lambda c: gw[:, c]).then_inc(m_full, 1)
            pe.wait_ge(cw_done, TT)
            for t in range(TT):
                last = pe.transpose(work[0][0:E, t * P:(t + 1) * P], cw[:, t], ident[:])
            last.then_inc(m_full, 1)
            pe.wait_ge(cwT_done, 1)
            pe.wait_ge(ld2[5], 16)
            pe.wait_ge(x_lo, TT)
            for t in range(TT):
                pe.matmul(yb[t][:], cwT[:, t * P:(t + 1) * P], b2s[:], start=True, stop=True).then_inc(m_full, 1)

            def hidden(e, p, first=False):
                s = p % 2
                pe.wait_ge(w1_lo, NP * e + p + 1)
                for f in range(FC):
                    n = FC * (NP * e + p) + f
                    if not first:
                        pe.wait_ge(h_relu, n - 3)
                    products(work[f][:], lambda i, c: w1s[i][:, s, c, f * P:(f + 1) * P],
                             lambda i, c: xT[i][:, c]).then_inc(h_full, 1)

            def second(e, p):
                s = p % 2
                pe.wait_ge(w2_lo, NP * e + p + 1)
                if p == 0:
                    pe.wait_ge(y_out, TT * (e + 1))
                for f in range(FC):
                    pe.wait_ge(h_lo, FC * (NP * e + p) + f + 1)
                    for t in range(TT):
                        for i, k in PASSES:
                            last = pe.matmul(yb[t][:], hs[i][:, s, f, t * P:(t + 1) * P], w2s[k][:, s, f],
                                             start=(p == 0 and f == 0 and (i, k) == (0, 0)),
                                             stop=(p == NP - 1 and f == FC - 1 and (i, k) == (1, 0)))
                last.then_inc(p2_used, 1)

            def expert(e, last=False):
                for p in range(NP):
                    if p < NP - 1:
                        hidden(e, p + 1)
                    elif not last:
                        hidden(e + 1, 0)
                    second(e, p)

            hidden(0, 0, True)
            with pe.Fori(0, LASTE) as e:
                expert(e)
            expert(LASTE, True)

        @block.vector
        def _(dve):
            steps = [0]

            def step(ins):
                ins.then_inc(chain, 1)
                steps[0] += 1

            def join():
                dve.wait_ge(chain, steps[0])

            def layer_norm(src, dst, signal, o):
                st = stat[:, 0:24].rearrange("p (t s) -> p t s", t=TT)
                mv = stat[:, 24:32].rearrange("p (t s) -> p t s", t=TT)
                for t in range(TT):
                    step(dve.bn_stats(st[:, t], src[:, t]))
                join()
                for t in range(TT):
                    step(dve.bn_aggr(mv[:, t], st[:, t]))
                join()
                v, root, y, z = (stat[:, c:c + TT] for c in (40, 44, 32, 48))
                dve.tensor_scalar(v, mv[:, :, 1], EPS, None, ALU.add).then_inc(var_done, 1)
                dve.wait_ge(root_done, o)
                for ins in (lambda: dve.reciprocal(y, root),
                            lambda: dve.tensor_tensor(z, y, y, ALU.mult),
                            lambda: dve.tensor_tensor(z, z, v, ALU.mult),
                            lambda: dve.tensor_scalar(z, z, -0.5, 1.5, ALU.mult, ALU.add),
                            lambda: dve.tensor_tensor(y, y, z, ALU.mult)):
                    step(ins())
                    join()
                for t in range(TT):
                    dve.tensor_scalar(dst[:, t], src[:, t], mv[:, t, 0:1], stat[:, 32 + t:33 + t],
                                      ALU.subtract, ALU.mult).then_inc(signal, 1)

            dve.wait_ge(ld_x, 16)
            layer_norm(xin, xin, ln1, 1)
            step(dve.memset(negmask[:, LK:LKP], LOWEST))

            def convert_mask(b):
                dve.wait_ge(ld_mask, 16 * (b + 1))
                dve.tensor_scalar(negmask[:, 0:LK], pr[:, 0, 0:LK].bitcast(I32), 0.0, LOWEST,
                                  ALU.is_gt, ALU.mult).then_inc(mask_done, 1)

            join()
            convert_mask(0)
            for i, w in enumerate((kw, vw)):
                dve.wait_ge(w_hi, i + 1)
                dve.tensor_tensor(w[1][:], wraw[:], w[0][:].bitcast(F32), ALU.subtract).then_inc(w_lo, 1)

            def key_lo(h, j, bank):
                k, m = j // 2, j % 2
                sl = slice(k * KC, (k + 1) * KC)
                col = C + 2 * h + m
                dve.scalar_tensor_tensor(out=kk[1][:, m, sl], in0=work[bank][:, 0:KC],
                                         scalar=biasT[:, col:col + 1], in1=kk[0][:, m, sl].bitcast(F32),
                                         op0=ALU.add, op1=ALU.subtract).then_inc(w_free, 1)

            def query_blocks(b, h):
                def parts(a):
                    rows = slice(HD * a, HD * (a + 1))
                    cols = slice((a % 2) * S, (a % 2 + 1) * S)
                    tok = slice(b * S, (b + 1) * S) if isinstance(b, int) else bass.ds(b * S, S)
                    return qT[rows, 2 * h:2 * h + 2, tok], [q[rows, :, a // 2, cols] for q in qbd]

                for a in range(HPC):
                    src, (hi, lo) = parts(a)
                    dve.tensor_copy(hi, src).then_inc(qbd_done, 1)
                own(dve, qbd_done, (2 * b + h) * 2 * HPC + HPC)
                for a in range(HPC):
                    src, (hi, lo) = parts(a)
                    dve.tensor_tensor(lo, src, hi.bitcast(F32), ALU.subtract).then_inc(qbd_done, 1)

            def item(b, last, step):
                kind, a, k = step
                i = ITEMS[last].index(step)
                bank = work[i % 4]
                if kind in "kv":
                    dve.wait_ge(kv_hi, NKV * b + FIRST_K + KV[last].index(step) + 1)
                if kind == "k":
                    key_lo(a, k, i % 4)
                elif kind == "v":
                    n = min(2, KT - 2 * k)
                    dve.tensor_tensor(vv[1][:, 2 * k:2 * k + n, :],
                                      bank[:, 0:n * 2 * P].rearrange("p (n d) -> p n d", n=n),
                                      vv[0][:, 2 * k:2 * k + n, :].bitcast(F32), ALU.subtract).then_inc(w_free, 1)
                elif kind == "s":
                    own(dve, w_full, count(b, last, step))
                    sl = slice(k * KC, (k + 1) * KC)
                    dve.tensor_tensor_reduce(pr[:, a % 4, sl], bank[:, 0:KC], negmask[:, sl], SCALE, LOWEST,
                                             ALU.add, ALU.max, smx[:, a, k:k + 1]).then_inc(w_free, 1)
                    if k == NKC - 1:
                        dve.wait_ge(w_free, count(b, last, step))
                        dve.tensor_reduce(nmx[:, a:a + 1], smx[:, a], AX.X, ALU.max,
                                          negate=True).then_inc(raw_nmx, 1)
                        own(dve, raw_nmx, 8 * b + a + 1)
                        dve.tensor_scalar(nmx[:, a:a + 1], nmx[:, a:a + 1], 1024.0, 1 / 1024.0,
                                          ALU.mult, ALU.mult).then_inc(nmx_done, 1)
                else:
                    dve.wait_ge(w_full, count(b, last, step))
                    dve.tensor_copy(recip[:, a % 2], bank[:, 0:2 * P]).then_inc(w_free, 1)

            def reciprocal(b, r):
                dve.wait_ge(exp_done, 8 * b + r + 1)
                dve.reciprocal(rinv[:, r:r + 1], rsum[:, r:r + 1]).then_inc(rinv_done, 1)
                dve.wait_ge(rinv_done, 8 * b + r + 1)
                dve.tensor_scalar(diag[:, r % 4], ident[:], rinv[:, r:r + 1], None, ALU.mult).then_inc(diag_done, 1)

            def pt_item(b, j):
                dve.wait_ge(pt_hi, NPT * b + j + 1)
                n = min(2, KT - 2 * (j % TPH))
                dve.tensor_tensor(pt[1][:, j % PTD, 0:n],
                                  ptp[j % PTD][:, 0:n * 2 * P].rearrange("p (n d) -> p n d", n=n),
                                  pt[0][:, j % PTD, 0:n].bitcast(F32), ALU.subtract).then_inc(pt_lo, 1)

            def group_out(b, last, g):
                dve.wait_ge(pt_used, NPT * b + TPH * (g + 1) + PTD)
                dve.wait_ge(w_free, count(b, last, ("r", g, 0)))
                for a in range(HPC):
                    rows, cols = slice(HD * a, HD * (a + 1)), slice(S * a, S * (a + 1))
                    tok = slice(b * S, (b + 1) * S) if isinstance(b, int) else bass.ds(b * S, S)
                    ins = dve.tensor_tensor(qT[rows, g, tok], pv[rows, cols], recip[rows, g % 2, cols], ALU.mult)
                ins.then_inc(pv_free, 1)

            def body(b, last=False):
                for step in STEPS[last]:
                    kind, a, j = step
                    if kind == "w":
                        lo, hi = (0, TPH + 2) if a % 2 == 0 else (TPH + 2, 2 * TPH)
                        for i in range(lo, hi):
                            pt_item(b, 2 * TPH * (a // 2) + i)
                        group_out(b, last, a)
                        continue
                    if kind == "r" and a % 2 == 0:
                        for r in range(2 * a, 2 * a + 4):
                            reciprocal(b, r)
                    item(b, last, step)
                    if step == ("s", 3, NKC - 1):
                        query_blocks(b, 1)
                    if step == ("s", 7, NKC - 1) and not last:
                        query_blocks(b + 1, 0)
                if not last:
                    convert_mask(b + 1)

            for j in range(FIRST_K):
                dve.wait_ge(kv_hi, j + 1)
                key_lo(0, j, j % 4)
            dve.wait_ge(q_done, C)
            dve.wait_ge(consts, 5)
            query_blocks(0, 0)
            dve.sem_inc(pt_lo, PTD)
            dve.sem_inc(pv_free, 1)
            dve.wait_ge(mask_done, 1)
            with dve.Fori(0, LASTB) as b:
                body(b)
                dve.wait_ge(mask_done, b + 2)
            body(LASTB, True)
            dve.wait_ge(pv_free, 4 * B + 1)
            dve.sem_inc(att_over, 1)

            dve.wait_ge(ld2[0], 16)
            for t in range(TT):
                dve.wait_ge(m_full, t + 1)
                step(dve.tensor_tensor(xs[:, t], xs[:, t], work[t][:], ALU.add))
            join()
            layer_norm(xs, hn, ln2, 2)
            dve.wait_ge(zeroed, 2)
            for t in range(TT):
                dve.wait_ge(m_full, 14 + t)
                for a in range(2):
                    r = slice(S * a, S * (a + 1))
                    dve.tensor_copy(pre[r, t, r], yb[t][r, r]).then_inc(pre_done, 1)
            for t in range(TT):
                dve.wait_ge(m_full, 18 + t)
                step(dve.tensor_tensor(xs[:, t], xs[:, t], work[t][:], ALU.add))
            join()
            layer_norm(xs, hn, ln2, 3)
            for t in range(TT):
                dve.wait_ge(x_hi, t + 1)
                cols = slice(t * P, (t + 1) * P)
                dve.tensor_tensor(xT[1][:, :, cols], yb[t][:].rearrange("p (c n) -> p c n", c=C),
                                  xT[0][:, :, cols].bitcast(F32), ALU.subtract).then_inc(x_lo, 1)
            dve.wait_ge(ld2[3], 16)
            for t in range(TT):
                dve.wait_ge(m_full, 26 + t)
                step(dve.tensor_tensor(logit[:, t], work[t][:, 0:E], gb[:], ALU.add))
            join()
            for t in range(TT):
                step(dve.max(top8[:, t], logit[:, t]))
            join()
            for t in range(TT):
                step(dve.max_index(idx8[:, t], top8[:, t], logit[:, t]))
            dve.tensor_tensor(wts[:, 0], top8[:, :, 1], top8[:, :, 0], ALU.subtract).then_inc(gate_diff, 1)
            join()
            step(dve.tensor_copy(idxf[:], idx8[:]))
            dve.wait_ge(gate_exp, 1)
            step(dve.tensor_scalar(wts[:, 0], wts[:, 1], 1.0, None, ALU.add))
            join()
            step(dve.reciprocal(wts[:, 2], wts[:, 0]))
            join()
            step(dve.tensor_tensor(wts[:, 3], wts[:, 1], wts[:, 2], ALU.mult))
            join()
            for t in range(TT):
                for k, dst in ((0, cw), (1, cw2)):
                    step(dve.tensor_scalar(dst[:, t], iota_e[:], idxf[:, t, k:k + 1], wts[:, 2 + k, t:t + 1],
                                           ALU.is_equal, ALU.mult))
            join()
            for t in range(TT):
                dve.tensor_tensor(cw[:, t], cw[:, t], cw2[:, t], ALU.add).then_inc(cw_done, 1)
            dve.wait_ge(m_full, 30)
            dve.tensor_copy(cwT[:], work[0][0:E, :]).then_inc(cwT_done, 1)
            for t in range(TT):
                dve.wait_ge(m_full, 31 + t)
                dve.tensor_tensor(xs[:, t], xs[:, t], yb[t][:], ALU.add).then_inc(y_out, 1)

            def w1_part(e, p):
                s = p % 2
                dve.wait_ge(w1_hi, NP * e + p + 1)
                dve.tensor_tensor(w1s[1][:, s], w1raw[:, s], w1s[0][:, s].bitcast(F32),
                                  ALU.subtract).then_inc(w1_lo, 1)

            def w2_part(e, p):
                s = p % 2
                dve.wait_ge(w2_hi, NP * e + p + 1)
                dve.tensor_tensor(w2s[1][:, s], w2raw[:, s], w2s[0][:, s].bitcast(F32),
                                  ALU.subtract).then_inc(w2_lo, 1)

            def add_expert(e):
                dve.wait_ge(p2_used, NP * (e + 1))
                dve.wait_ge(y_out, TT * (e + 1))
                for t in range(TT):
                    col = cw[:, t, e:e + 1] if isinstance(e, int) else cw[:, t, bass.ds(e, 1)]
                    dve.scalar_tensor_tensor(out=xs[:, t], in0=yb[t][:], scalar=col, in1=xs[:, t],
                                             op0=ALU.mult, op1=ALU.add).then_inc(y_out, 1)

            def expert(e, first=False, last=False):
                for p in range(NP):
                    if p < NP - 1:
                        w1_part(e, p + 1)
                    elif not last:
                        w1_part(e + 1, 0)
                    w2_part(e, p)
                    for f in range(FC):
                        n = FC * (NP * e + p) + f
                        dve.wait_ge(h_hi, n + 1)
                        dve.tensor_tensor(hs[1][:, p % 2, f], hf[:, f % 2], hs[0][:, p % 2, f].bitcast(F32),
                                          ALU.subtract).then_inc(h_lo, 1)
                    if p == 0 and not first:
                        add_expert(e - 1)

            w1_part(0, 0)
            expert(0, first=True)
            with dve.Fori(1, LASTE) as e:
                expert(e)
            expert(LASTE, last=True)
            add_expert(LASTE)


def kernel(**inputs):
    import numpy as np
    import concourse.bacc as bacc
    from concourse.bass_utils import run_bass_kernel_spmd

    def a(name):
        return np.asarray(inputs[name])

    ctxT = np.zeros((B, D, KP), np.float32)
    ctxT[:, :, :LK] = a("ctx_1024").transpose(0, 2, 1)
    arrays = {
        "x": a("x").reshape(T, D), "ctxT": ctxT, "mask": a("mask_BxS2_ik0"),
        "qwT": a("L0_xattn_q_w").T, "kwT": a("L0_xattn_k_w").T, "vwT": a("L0_xattn_v_w").T,
        "wqT": a("L0_attn_W_q").T,
        "bias3": np.concatenate([a("L0_xattn_q_b"), a("L0_xattn_k_b"), a("L0_xattn_v_b")]).reshape(3 * C, P),
        "gate_w": a("L0_ffn_gate_w"), "gate_b": a("L0_ffn_gate_b").reshape(1, E),
        "w1": a("L0_ffn_w1"), "b1": a("L0_ffn_b1"), "w2": a("L0_ffn_w2"), "b2": a("L0_ffn_b2"),
    }
    arrays = {f"in_{n}": np.ascontiguousarray(v) for n, v in arrays.items()}
    nc = bacc.Bacc("TRN2", target_bir_lowering=False, num_devices=1)
    args = [nc.dram_tensor(n, v.shape, mybir.dt.from_np(v.dtype), kind="ExternalInput").ap()
            for n, v in arrays.items()]
    out = nc.dram_tensor("out", (T, D), F32, kind="ExternalOutput").ap()
    layer(nc, *args, out)
    r = run_bass_kernel_spmd(nc, [arrays], core_ids=[0])
    return r.results[0]["out"].reshape(B, S, D)
```

```python
from contextlib import ExitStack

import concourse.bass as bass
from concourse import mybir

ALU = mybir.AluOpType
ACT = mybir.ActivationFunctionType
AX = mybir.AxisListType
F32 = mybir.dt.float32
F32R = mybir.dt.float32r
BF16 = mybir.dt.bfloat16
I32 = mybir.dt.int32
U32 = mybir.dt.uint32

P = 128
BANK = 512
B, S, D = 8, 64, 512
T = B * S
TT = T // P
C = D // P
LK = 1601
HD = 32
HPC = P // HD
KT = -(-LK // P)
KP = KT * P
KC = 402
NKC = 4
LKP = KC * NKC
CC = KP // NKC
E, F = 8, 2048
NP = F // 512
FC = 4
HB = FC // 2
SLOTS = 256
ST = SLOTS // P
BLOCKS = T // SLOTS
SCALE = float(HD) ** -0.5
EPS = 1e-5
LOWEST = -3.0e38


def steps_of(last):
    steps = []
    for h in range(2):
        v = [("v", h, j) for j in range((KT + 1) // 2)]
        k = [] if h and last else [("k", 1 - h, j) for j in range(2 * NKC)]
        steps += v[:3]
        for r in range(4):
            steps += [("s", 4 * h + r, j) for j in range(NKC)] + v[3 + r:4 + r]
        steps += k[:6] + [("r", 2 * h, 0), ("r", 2 * h + 1, 0)] + k[6:7]
        steps += [("w", 2 * h, 0)] + k[7:] + [("w", 2 * h + 1, 0)]
    return steps


STEPS = [steps_of(False), steps_of(True)]
ITEMS = [[s for s in steps if s[0] != "w"] for steps in STEPS]
KV = [[s for s in items if s[0] in "kv"] for items in ITEMS]
NW = len(ITEMS[0])
NKV = len(KV[0])
FIRST_K = 2 * NKC
NPT = 2 * (KT + 1)
PTD = 3
TPH = KT // 2 + 1


def count(b, last, step):
    return NW * b + FIRST_K + ITEMS[last].index(step) + 1


def before_bank(b, i):
    return NW * b + FIRST_K + (i - 3 if i >= 4 else (-1, 0, -1, 0)[i])


def pt_before(j):
    last = j - PTD if j >= PTD else max(m for m in range(NPT) if m % PTD == j) - NPT
    return last + 1 + PTD


def layer(nc, x, ctxT, mask, qwT, kwT, vwT, wqT, bias3, gate_w, gate_b, w1, b1, w2, b2, out):
    with ExitStack() as top:
        def sem(name):
            return top.enter_context(nc.semaphore(name))

        def sb(stack, name, shape, dt):
            return stack.enter_context(nc.sbuf_tensor(name, shape, dt))

        work = [top.enter_context(nc.psum_tensor(f"work{i}", [P, BANK], F32)) for i in range(4)]
        ptp = [top.enter_context(nc.psum_tensor(f"ptp{i}", [P, BANK], F32)) for i in range(3)]
        pv = top.enter_context(nc.psum_tensor("pv", [P, BANK], F32))

        ident = sb(top, "ident", [P, P], F32)
        ones = sb(top, "ones", [P, P], F32)
        qT = sb(top, "qT", [P, C, T], F32)
        biasT = sb(top, "biasT", [P, 3 * C], F32)
        stat = sb(top, "stat", [P, 64], F32)

        with ExitStack() as m:
            kw = [sb(m, f"kw_{n}", [P, C, D], F32R) for n in ("hi", "lo")]
            vw = [sb(m, f"vw_{n}", [P, C, D], F32R) for n in ("hi", "lo")]
            cx = [sb(m, f"cx_{n}", [P, C, KP], F32R) for n in ("hi", "lo")]
            kk = [sb(m, f"kk_{n}", [P, 2, LKP], F32R) for n in ("hi", "lo")]
            pr = sb(m, "pr", [P, 4, KP], F32)
            negmask = sb(m, "negmask", [P, LKP], BF16)
            raw = sb(m, "raw", [P, 2, C, CC], F32)
            qbd = [sb(m, f"qbd_{n}", [P, 2, 2, P], F32R) for n in ("hi", "lo")]
            diag = sb(m, "diag", [P, 4, P], F32)
            recip = sb(m, "recip", [P, 2, 2 * P], F32)
            smx = sb(m, "smx", [P, 8, NKC], F32)
            nmx = sb(m, "nmx", [P, 8], F32)
            rsum = sb(m, "rsum", [P, 8], F32)
            rinv = sb(m, "rinv", [P, 8], F32)
            with ExitStack() as m2:
                vv = [sb(m2, f"vv_{n}", [P, KT, 2 * P], F32R) for n in ("hi", "lo")]
                pt = [sb(m2, f"pt_{n}", [P, PTD, 2, 2 * P], F32R) for n in ("hi", "lo")]
            xin = sb(m, "xin", [P, TT, D], F32)
            xnT = sb(m, "xnT", [P, C, T], F32)
            wraw = sb(m, "wraw", [P, C, D], F32)
            brow = sb(m, "brow", [3 * C, P], F32)

        with ExitStack() as m:
            xs = sb(m, "xs", [P, TT, D], F32)
            hn = sb(m, "hn", [P, TT, D], F32)
            hT = sb(m, "hT", [P, C, T], F32)
            gw = sb(m, "gw", [P, C, E], F32)
            gb = sb(m, "gb", [P, TT, E], F32)
            b1r = sb(m, "b1r", [P, P], F32)
            b1T = sb(m, "b1T", [P, P], F32)
            b2s = sb(m, "b2s", [E, D], F32)
            logit = sb(m, "logit", [P, TT, E], F32)
            top8 = sb(m, "top8", [P, TT, 8], F32)
            idx8 = sb(m, "idx8", [P, TT, 8], U32)
            idxf = sb(m, "idxf", [P, TT, 8], F32)
            iota_e = sb(m, "iota_e", [P, TT, E], F32)
            iota_s = sb(m, "iota_s", [P, SLOTS], F32)
            slot_id = sb(m, "slot_id", [P, BLOCKS, ST], F32)
            before = sb(m, "before", [P, P], F32)
            wts = sb(m, "wts", [P, 4, TT], F32)
            best = sb(m, "best", [P, 2, TT, E], F32)
            chosen = sb(m, "chosen", [P, TT, E], F32)
            place = sb(m, "place", [P, TT, BLOCKS * E], F32)
            total = sb(m, "total", [P, 4], F32)
            crowded = sb(m, "crowded", [P, 1], I32)
            cw = sb(m, "cw", [P, TT, E], F32)
            cw2 = sb(m, "cw2", [P, TT, E], F32)
            cwT = sb(m, "cwT", [E, T], F32)
            placeT = sb(m, "placeT", [E, T], F32)
            place_e = sb(m, "place_e", [E, T], F32R)
            ones_e = sb(m, "ones_e", [E, P], F32R)
            xn = [sb(m, f"xn_{n}", [P, TT, D], F32R) for n in ("hi", "lo")]
            w1raw = sb(m, "w1raw", [P, 2, C, 512], F32)
            w2raw = sb(m, "w2raw", [P, 2, FC, D], F32)
            w1s = [sb(m, f"w1_{n}", [P, 2, C, 512], F32R) for n in ("hi", "lo")]
            hf = sb(m, "hf", [P, FC, SLOTS], F32)
            hs = [sb(m, f"h_{n}", [P, 2, FC, SLOTS], F32R) for n in ("hi", "lo")]
            xg = [sb(m, f"xg_{n}", [P, C, SLOTS], F32R) for n in ("hi", "lo")]
            pick = sb(m, "pick", [P, TT, SLOTS], F32R)
            put = sb(m, "put", [P, ST, T], F32R)
            ys = [sb(m, f"y_{n}", [P, ST, D], F32R) for n in ("hi", "lo")]
            with ExitStack() as m2:
                w2s = [sb(m2, f"w2_{n}", [P, 2, FC, D], F32R) for n in ("hi", "lo")]
            wq2 = sb(m, "wq2", [P, C, D], F32)
            gT = sb(m, "gT", [P, C, T], F32)
            pre = sb(m, "pre", [P, TT, P], F32)

        ld_x, ld_b, ld_w = sem("x_loaded"), sem("biases_loaded"), [sem(f"weight{i}_loaded") for i in range(3)]
        ld_raw = [sem(f"context_chunk_loaded{i}") for i in range(2)]
        ld_mask = sem("mask_loaded")
        consts = sem("constants_ready")
        chain = sem("vector_step")
        ln1 = sem("x_normalised")
        var_done, root_done = sem("variance_ready"), sem("root_ready")
        t_full = sem("pre_psum_full")
        t_out = sem("pre_psum_drained")
        w_hi, w_lo = sem("weight_hi"), sem("weight_lo")
        c_hi, c_lo = sem("context_hi"), sem("context_lo")
        q_done = sem("queries_ready")
        qbd_done = sem("query_blocks_ready")
        w_full = sem("work_bank_full")
        kv_hi = sem("keys_values_hi")
        w_free = sem("work_bank_drained")
        raw_nmx = sem("raw_row_maximum")
        nmx_done = sem("row_maximum_ready")
        exp_done = sem("row_exponentials_ready")
        rinv_done = sem("row_reciprocal")
        diag_done = sem("reciprocal_diagonal_ready")
        pt_full, pt_hi, pt_lo = sem("probabilities_transposed"), sem("probabilities_hi"), sem("probabilities_lo")
        pt_used = sem("probabilities_used")
        pv_free = sem("weighted_values_drained")
        mask_done = sem("mask_ready")
        att_over = sem("attention_over")
        ld2 = [sem(f"late_load{i}") for i in range(6)]
        zeroed = sem("late_constants_ready")
        ob_done = sem("attention_bias_added")
        m_full, m_out = sem("mid_psum_full"), sem("mid_psum_copied")
        x_add, ln2 = sem("residual_added"), sem("residual_normalised")
        pre_done = sem("self_scores_ready")
        gate_diff, gate_exp = sem("gate_difference"), sem("gate_exponential")
        x_hi, x_lo = sem("moe_input_hi"), sem("moe_input_lo")
        chosen_done, place_done = sem("choice_ready"), sem("places_ready")
        placeT_done, flag_done = sem("places_transposed"), sem("crowded_ready")
        pick_done, xg_full, xg_hi, xg_lo = sem("pick_ready"), sem("gathered"), sem("gathered_hi"), sem("gathered_lo")
        row_done, row_full, put_done = sem("expert_places_ready"), sem("places_broadcast"), sem("put_ready")
        y_hi, y_lo, y_put = sem("output_hi"), sem("output_lo"), sem("output_scattered")
        result_done = sem("result_ready")
        cw_done, cwT_done = sem("expert_weights_ready"), sem("expert_weights_transposed")
        ld_w1 = [sem(f"w1_loaded{i}") for i in range(2)]
        ld_w2 = [sem(f"w2_loaded{i}") for i in range(2)]
        w1_hi, w1_lo, w2_hi, w2_lo = sem("w1_hi"), sem("w1_lo"), sem("w2_hi"), sem("w2_lo")
        h_full, h_relu, h_hi, h_lo = sem("hidden_full"), sem("hidden_relu"), sem("hidden_hi"), sem("hidden_lo")
        p2_used = sem("w2_piece_used")
        y_out = sem("expert_output_added")
        stored = sem("output_stored")

        LASTB, LASTE = B - 1, E - 1
        yb = ptp + [pv]
        block = top.enter_context(nc.Block())

        def own(eng, sem, value):
            eng.wait_ge(sem, value)
            if not isinstance(value, int):
                eng.nop(nofuse=True)

        def overflow(eng, experts):
            eng.wait_ge(flag_done, 1)
            with eng.If(eng.value_load(crowded[0:1, 0:1], min_val=0, max_val=1) > 0):
                experts(1)
                eng.nop(nofuse=True)

        @block.sync
        def _(sp):
            sp.dma_start(xin[:], x.rearrange("(t p) d -> p t d", p=P)).then_inc(ld_x, 16)
            sp.dma_start(brow[:], bias3).then_inc(ld_b, 16)
            sp.dma_start(wraw[:], qwT.rearrange("(c p) n -> p c n", p=P)).then_inc(ld_w[0], 16)

            def load_chunk(b, k, first=False):
                if not first:
                    own(sp, c_lo, NKC * b + k - 1)
                src = ctxT[b:b + 1] if isinstance(b, int) else ctxT[bass.ds(b, 1)]
                sp.dma_start(raw[:, k % 2], src[:, :, k * CC:(k + 1) * CC].rearrange(
                    "o (c p) n -> p (o c) n", p=P)).then_inc(ld_raw[k % 2], 16)

            def load_mask(b):
                src = mask[b:b + 1, :] if isinstance(b, int) else mask[bass.ds(b, 1), :]
                sp.dma_start(pr[:, 0, 0:LK].bitcast(I32), src.broadcast_to([P, LK])).then_inc(ld_mask, 16)

            load_chunk(0, 0, True)
            load_chunk(0, 1, True)
            load_mask(0)
            sp.wait_ge(t_full, 2 * C + 1)
            sp.dma_start(wraw[:], kwT.rearrange("(c p) n -> p c n", p=P)).then_inc(ld_w[1], 16)
            sp.wait_ge(w_lo, 1)
            sp.dma_start(wraw[:], vwT.rearrange("(c p) n -> p c n", p=P)).then_inc(ld_w[2], 16)
            load_chunk(0, 2)
            load_chunk(0, 3)

            with sp.Fori(0, LASTB) as b:
                for k in range(NKC):
                    load_chunk(b + 1, k)
                own(sp, pt_full, NPT * b + 3 * TPH)
                load_mask(b + 1)

            sp.wait_ge(att_over, 4)
            sp.dma_start(xs[:], x.rearrange("(t p) d -> p t d", p=P)).then_inc(ld2[0], 16)
            sp.dma_start(b1r[:], b1.rearrange("e (k j) -> (e k) j", j=P)).then_inc(ld2[4], 16)
            sp.dma_start(wq2[:], wqT.rearrange("(c p) n -> p c n", p=P)).then_inc(ld2[1], 16)
            sp.dma_start(gw[:], gate_w.rearrange("(c p) n -> p c n", p=P)).then_inc(ld2[2], 16)
            sp.dma_start(gb[:], gate_b.broadcast_to([P, TT * E])).then_inc(ld2[3], 16)
            sp.dma_start(b2s[:], b2).then_inc(ld2[5], 16)

            def load_w1(ph, e, p, first=False):
                s, n = p % 2, e + E * ph
                if not first:
                    own(sp, w1_lo, NP * n + p - 1)
                src = w1[e:e + 1] if isinstance(e, int) else w1[bass.ds(e, 1)]
                sp.dma_start(w1raw[:, s], src[:, :, p * 512:(p + 1) * 512].rearrange(
                    "o (c p) n -> p (o c) n", p=P)).then_inc(ld_w1[s], 16)

            def load_w2(ph, e, p, first=False):
                s, n = p % 2, e + E * ph
                if not first:
                    own(sp, w2_lo, NP * n + p - 1)
                src = w2[e:e + 1] if isinstance(e, int) else w2[bass.ds(e, 1)]
                sp.dma_start(w2raw[:, s], src[:, p * 512:(p + 1) * 512, :].rearrange(
                    "o (c p) n -> p (o c) n", p=P)).then_inc(ld_w2[s], 16)

            def expert(ph, e, fresh=False, last=False):
                for p in range(NP):
                    if p < NP - 1:
                        load_w1(ph, e, p + 1, fresh and p == 0)
                    elif not last:
                        load_w1(ph, e + 1, 0)
                    load_w2(ph, e, p, fresh and p < 2)

            def experts(ph):
                load_w1(ph, 0, 0, ph == 0)
                expert(ph, 0, ph == 0)
                with sp.Fori(1, LASTE) as e:
                    expert(ph, e)
                expert(ph, LASTE, last=True)

            experts(0)
            overflow(sp, experts)
            sp.wait_ge(result_done, 1)
            sp.dma_start(out.rearrange("(t p) d -> p t d", p=P), xs[:]).then_inc(stored, 16)
            sp.wait_ge(stored, 16)

        @block.gpsimd
        def _(pool):
            pool.memset(ident[:], 0.0).then_inc(consts, 1)
            pool.memset(ones[:], 1.0).then_inc(consts, 1)
            pool.wait_ge(consts, 2)
            pool.affine_select(out=ident[:], in_=ident[:], compare_op=ALU.not_equal, fill=1.0, base=0,
                               pattern=[[-1, P]], channel_multiplier=1).then_inc(consts, 1)
            for q in qbd:
                pool.memset(q[:].bitcast(F32), 0.0).then_inc(consts, 1)
            pool.memset(pr[:, :, LKP:KP], 0.0).then_inc(consts, 1)
            pool.wait_ge(consts, 6)

            def ctx_lo(b, k):
                own(pool, c_hi, NKC * b + k + 1)
                sl = slice(k * CC, (k + 1) * CC)
                pool.tensor_tensor(cx[1][:, :, sl], raw[:, k % 2], cx[0][:, :, sl].bitcast(F32),
                                   ALU.subtract).then_inc(c_lo, 1)

            for k in range(NKC):
                ctx_lo(0, k)
            with pool.Fori(1, B) as b:
                for k in range(NKC):
                    ctx_lo(b, k)
            pool.wait_ge(c_lo, NKC * B)
            pool.sem_inc(att_over, 1)

            pool.wait_ge(att_over, 4)
            pool.memset(pre[:], 0.0).then_inc(zeroed, 1)
            pool.iota(iota_e[:], pattern=[[0, TT], [1, E]], base=0, channel_multiplier=0,
                      allow_small_or_imprecise_dtypes=True).then_inc(zeroed, 1)
            pool.iota(iota_s[:], pattern=[[1, SLOTS]], base=1, channel_multiplier=0,
                      allow_small_or_imprecise_dtypes=True).then_inc(zeroed, 1)
            pool.iota(slot_id[:], pattern=[[SLOTS, BLOCKS], [P, ST]], base=1, channel_multiplier=1,
                      allow_small_or_imprecise_dtypes=True).then_inc(zeroed, 1)
            pool.affine_select(out=before[:], in_=ones[:], compare_op=ALU.is_gt, fill=0.0, base=0,
                               pattern=[[1, P]], channel_multiplier=-1).then_inc(zeroed, 1)
            for t in range(TT):
                pool.wait_ge(x_hi, t + 1)
                pool.tensor_tensor(xn[1][:, t], hn[:, t], xn[0][:, t].bitcast(F32), ALU.subtract).then_inc(x_lo, 1)

            def expert(ph, e, fresh=False):
                n = e + E * ph
                for p in range(NP):
                    if not (fresh and p < 2):
                        own(pool, p2_used, NP * n + p - 1)
                    for f in range(FC):
                        own(pool, h_relu, FC * (NP * n + p) + f + 1)
                        pool.tensor_copy(hs[0][:, p % 2, f], hf[:, f]).then_inc(h_hi, 1)

            def experts(ph):
                expert(ph, 0, ph == 0)
                with pool.Fori(1, E) as e:
                    expert(ph, e)

            experts(0)
            overflow(pool, experts)

        @block.scalar
        def _(act):
            def copy(dst, src, signal):
                act.activation(dst, src, ACT.Copy).then_inc(signal, 1)

            def ctx_hi(b, k):
                act.wait_ge(ld_raw[k % 2], 16 * (2 * b + k // 2 + 1))
                copy(cx[0][:, :, k * CC:(k + 1) * CC], raw[:, k % 2], c_hi)

            def root(o):
                act.wait_ge(var_done, o)
                act.activation(stat[:, 44:48], stat[:, 40:44], ACT.Sqrt).then_inc(root_done, 1)

            root(1)
            ctx_hi(0, 0)
            ctx_hi(0, 1)
            for c in range(C):
                act.wait_ge(t_full, c + 1)
                copy(xnT[:, c], work[c][:], t_out)
            act.wait_ge(t_full, C + 1)
            copy(biasT[:], pv[:, 0:3 * C], t_out)
            act.wait_ge(t_out, C + 1)
            for c in range(C):
                act.wait_ge(t_full, C + 2 + c)
                act.activation(qT[:, c], work[c][:], ACT.Identity, bias=biasT[:, c:c + 1]).then_inc(q_done, 1)
            for i, w in enumerate((kw, vw)):
                act.wait_ge(ld_w[1 + i], 16)
                copy(w[0][:], wraw[:], w_hi)
            ctx_hi(0, 2)
            ctx_hi(0, 3)

            def key_hi(h, j, bank):
                k, m = j // 2, j % 2
                act.activation(kk[0][:, m, k * KC:(k + 1) * KC], work[bank][:, 0:KC], ACT.Identity,
                               bias=biasT[:, C + 2 * h + m:C + 2 * h + m + 1]).then_inc(kv_hi, 1)

            def kv_item(b, last, step):
                kind, h, j = step
                bank = ITEMS[last].index(step) % 4
                act.wait_ge(w_full, count(b, last, step))
                if kind == "k":
                    key_hi(h, j, bank)
                else:
                    n = min(2, KT - 2 * j)
                    copy(vv[0][:, 2 * j:2 * j + n, :],
                         work[bank][:, 0:n * 2 * P].rearrange("p (n d) -> p n d", n=n), kv_hi)

            for j in range(FIRST_K):
                act.wait_ge(w_full, j + 1)
                key_hi(0, j, j % 4)

            def exponentials(b, r):
                act.wait_ge(nmx_done, 8 * b + r + 1)
                row = pr[:, r % 4, 0:LKP]
                act.activation(row, row, ACT.Exp, bias=nmx[:, r:r + 1],
                               accum_out=rsum[:, r:r + 1]).then_inc(exp_done, 1)

            def pt_item(b, j):
                act.wait_ge(pt_full, NPT * b + j + 1)
                act.wait_ge(pt_used, NPT * b + pt_before(j))
                n = min(2, KT - 2 * (j % TPH))
                copy(pt[0][:, j % PTD, 0:n], ptp[j % PTD][:, 0:n * 2 * P].rearrange("p (n d) -> p n d", n=n), pt_hi)

            LAST_READ = {(CC * (k + 1) - 1) // (2 * P): k for k in range(NKC)}

            def body(b, last=False):
                for step in STEPS[last]:
                    kind, a, j = step
                    if kind in "kv":
                        kv_item(b, last, step)
                    if kind == "v" and a == 1 and j in LAST_READ and not last:
                        ctx_hi(b + 1, LAST_READ[j])
                    if kind == "v" and j >= 3:
                        exponentials(b, 4 * a + j - 3)
                    if kind == "w":
                        lo, hi = (0, TPH + 2) if a % 2 == 0 else (TPH + 2, 2 * TPH)
                        for i in range(lo, hi):
                            pt_item(b, 2 * TPH * (a // 2) + i)

            with act.Fori(0, LASTB) as b:
                body(b)
            body(LASTB, True)
            act.wait_ge(pt_hi, NPT * B)
            act.sem_inc(att_over, 1)

            act.wait_ge(att_over, 4)
            for c in range(C):
                act.activation(qT[:, c], qT[:, c], ACT.Identity,
                               bias=biasT[:, 2 * C + c:2 * C + c + 1]).then_inc(ob_done, 1)
            act.wait_ge(m_full, 5)
            copy(b1T[:], pv[:, 0:P], m_out)
            root(2)
            for t in range(TT):
                act.wait_ge(m_full, 6 + t)
                copy(hT[:, :, t * P:(t + 1) * P], yb[t][:].rearrange("p (c n) -> p c n", c=C), m_out)
            for c in range(C):
                act.wait_ge(m_full, 10 + c)
                copy(gT[:, c], work[c][:], m_out)
            root(3)

            def w1_part(ph, e, p, fresh=False):
                s, n = p % 2, e + E * ph
                act.wait_ge(ld_w1[s], 16 * (2 * n + p // 2 + 1))
                if not fresh:
                    act.wait_ge(h_full, HB * (NP * n + p - 1))
                copy(w1s[0][:, s], w1raw[:, s], w1_hi)

            def w2_part(ph, e, p, fresh=False):
                s, n = p % 2, e + E * ph
                act.wait_ge(ld_w2[s], 16 * (2 * n + p // 2 + 1))
                if not fresh:
                    act.wait_ge(p2_used, NP * n + p - 1)
                copy(w2s[0][:, s], w2raw[:, s], w2_hi)

            def gathered(n):
                for i in range(2):
                    act.wait_ge(xg_full, 2 * n + i + 1)
                    copy(xg[0][:, 2 * i:2 * i + 2], work[2 + i][:].rearrange("p (c n) -> p c n", c=2), xg_hi)

            def outputs(n):
                act.wait_ge(p2_used, NP * (n + 1))
                if not (isinstance(n, int) and n == 0):
                    act.wait_ge(y_put, TT * n)
                for i in range(ST):
                    copy(ys[0][:, i], yb[i][:], y_hi)

            def expert(ph, e, fresh=False, first=False, last=False):
                n = e + E * ph
                for p in range(NP):
                    if p < NP - 1:
                        w1_part(ph, e, p + 1, fresh and p == 0)
                    elif not last:
                        w1_part(ph, e + 1, 0)
                    w2_part(ph, e, p, fresh and p < 2)
                    for f in range(FC):
                        c = FC * (NP * n + p) + f
                        if f % 2 == 0:
                            act.wait_ge(h_full, HB * (NP * n + p) + f // 2 + 1)
                        if not (fresh and p == 0):
                            act.wait_ge(h_lo, c - 3)
                        col = 16 * e + FC * p + f
                        bias = b1T[:, col:col + 1] if isinstance(e, int) else b1T[:, bass.ds(col, 1)]
                        act.activation(hf[:, f], work[f // 2][:, (f % 2) * SLOTS:(f % 2 + 1) * SLOTS],
                                       ACT.Relu, bias=bias).then_inc(h_relu, 1)
                    if p == 0 and not first:
                        outputs(n - 1)
                if not last:
                    gathered(n + 1)

            def experts(ph):
                if ph:
                    w1_part(ph, 0, 0)
                gathered(E * ph)
                expert(ph, 0, ph == 0, first=True)
                with act.Fori(1, LASTE) as e:
                    expert(ph, e)
                expert(ph, LASTE, last=True)
                outputs(E * ph + LASTE)

            w1_part(0, 0, 0, True)
            for t in range(TT):
                act.wait_ge(ln2, TT + t + 1)
                copy(xn[0][:, t], hn[:, t], x_hi)
                if t % 2:
                    for u in (t - 1, t):
                        act.wait_ge(m_full, 22 + u)
                        copy(hT[:, :, u * P:(u + 1) * P], yb[u][:].rearrange("p (c n) -> p c n", c=C), m_out)
            act.wait_ge(gate_diff, 1)
            act.activation(wts[:, 1], wts[:, 0], ACT.Exp).then_inc(gate_exp, 1)
            experts(0)
            overflow(act, experts)

        @block.tensor
        def _(pe):
            PASSES = ((0, 0), (0, 1), (1, 0))

            def products(dst, lhs, rhs, n=C):
                for c in range(n):
                    for i, j in PASSES:
                        last = pe.matmul(dst, lhs(i, c), rhs(j, c), start=(c == 0 and (i, j) == (0, 0)),
                                         stop=(c == n - 1 and (i, j) == (1, 0)))
                return last

            def plain(dst, lhs, rhs, n=C):
                for c in range(n):
                    last = pe.matmul(dst, lhs(c), rhs(c), start=(c == 0), stop=(c == n - 1))
                return last

            pe.wait_ge(consts, 3)
            pe.wait_ge(ln1, TT)
            for c in range(C):
                for t in range(TT):
                    last = pe.transpose(work[c][:, t * P:(t + 1) * P], xin[:, t, c * P:(c + 1) * P], ident[:])
                last.then_inc(t_full, 1)
            pe.wait_ge(ld_b, 16)
            pe.transpose(pv[:, 0:3 * C], brow[:], ident[0:3 * C, 0:3 * C]).then_inc(t_full, 1)
            pe.wait_ge(t_out, C + 1)
            pe.wait_ge(ld_w[0], 16)
            for m_ in range(C):
                plain(work[m_][:], lambda c: wraw[:, c, m_ * P:(m_ + 1) * P],
                      lambda c: xnT[:, c]).then_inc(t_full, 1)

            def key_item(b, h, j, bank):
                k, m = j // 2, j % 2
                if m == 0:
                    pe.wait_ge(c_lo, NKC * b + k + 1)
                products(work[bank][:, 0:KC], lambda i, c: kw[i][:, c, (2 * h + m) * P:(2 * h + m + 1) * P],
                         lambda i, c: cx[i][:, c, k * KC:(k + 1) * KC]).then_inc(w_full, 1)

            def value_item(h, j, bank):
                for n in range(min(2, KT - 2 * j)):
                    kt = 2 * j + n
                    last = products(work[bank][:, n * 2 * P:(n + 1) * 2 * P],
                                    lambda i, c: cx[i][:, c, kt * P:(kt + 1) * P],
                                    lambda i, c: vw[i][:, c, h * 2 * P:(h + 1) * 2 * P])
                last.then_inc(w_full, 1)

            def item(b, last, step):
                kind, a, k = step
                i = ITEMS[last].index(step)
                bank = work[i % 4]
                pe.wait_ge(w_free, before_bank(b, i))
                if kind == "k":
                    key_item(b + 1 if a == 0 else b, a, k, i % 4)
                elif kind == "v":
                    value_item(a, k, i % 4)
                elif kind == "s":
                    cc, rt = (a % 4) // 2, a % 2
                    if a % 4 == 0 and k == 0:
                        pe.wait_ge(qbd_done, (2 * b + a // 4 + 1) * 2 * HPC)
                    products(bank[:, 0:KC], lambda i_, c: qbd[i_][:, cc, rt, :],
                             lambda i_, c: kk[i_][:, cc, k * KC:(k + 1) * KC], 1).then_inc(w_full, 1)
                else:
                    pe.wait_ge(diag_done, 8 * b + 2 * a + 2)
                    for rt in range(2):
                        last_mm = pe.matmul(bank[:, rt * P:(rt + 1) * P], ones[:],
                                            diag[:, 2 * (a % 2) + rt], start=True, stop=True)
                    last_mm.then_inc(w_full, 1)

            pe.wait_ge(q_done, C)
            pe.wait_ge(w_lo, 1)
            for j in range(FIRST_K):
                if j >= 4:
                    pe.wait_ge(w_free, j - 3)
                key_item(0, 0, j, j % 4)
            pe.wait_ge(w_lo, 2)
            pe.sem_inc(pt_used, PTD)

            def turn(b, j):
                g, first = j // TPH, 2 * (j % TPH)
                pe.wait_ge(pt_lo, NPT * b + pt_before(j))
                if j % TPH == 0:
                    pe.wait_ge(exp_done, 8 * b + 2 * g + 2)
                for n in range(min(2, KT - first)):
                    for rt in range(2):
                        last = pe.transpose(ptp[j % PTD][:, (2 * n + rt) * P:(2 * n + rt + 1) * P],
                                            pr[:, (2 * g + rt) % 4, (first + n) * P:(first + n + 1) * P], ident[:])
                last.then_inc(pt_full, 1)

            def weigh(b, j):
                g, first = j // TPH, 2 * (j % TPH)
                pe.wait_ge(pt_lo, NPT * b + j + 1 + PTD)
                if first == 0:
                    pe.wait_ge(pv_free, 4 * b + g + 1)
                for n in range(min(2, KT - first)):
                    kt = first + n
                    for i, k in PASSES:
                        last = pe.matmul(pv[:, 0:2 * P], vv[i][:, kt, (g % 2) * P:(g % 2 + 1) * P],
                                         pt[k][:, j % PTD, n], start=(kt == 0 and (i, k) == (0, 0)),
                                         stop=(kt == KT - 1 and (i, k) == (1, 0)))
                last.then_inc(pt_used, 1)

            def weighted(b, last, g):
                first, end = 2 * TPH * (g // 2), 2 * TPH * (g // 2 + 1)
                if g % 2 == 0:
                    pe.wait_ge(w_free, count(b, last, ("v", g // 2, TPH - 1)))
                    turn(b, first)
                    turn(b, first + 1)
                for j in range(TPH * g, TPH * (g + 1)):
                    if j + 2 < end:
                        turn(b, j + 2)
                    weigh(b, j)

            def body(b, last=False):
                for step in STEPS[last]:
                    if step[0] == "w":
                        weighted(b, last, step[1])
                    else:
                        item(b, last, step)

            with pe.Fori(0, LASTB) as b:
                body(b)
            body(LASTB, True)
            pe.sem_inc(att_over, 1)

            pe.wait_ge(ob_done, C)
            for t in range(TT):
                for c in range(C):
                    last = pe.transpose(work[t][:, c * P:(c + 1) * P], qT[:, c, t * P:(t + 1) * P], ident[:])
                last.then_inc(m_full, 1)
            pe.wait_ge(ld2[4], 16)
            pe.transpose(pv[:, 0:P], b1r[:], ident[:]).then_inc(m_full, 1)

            def turn_tiles(k):
                for t in range(TT):
                    pe.wait_ge(ln2, k * TT + t + 1)
                    for c in range(C):
                        last = pe.transpose(yb[t][:, c * P:(c + 1) * P], hn[:, t, c * P:(c + 1) * P], ident[:])
                    last.then_inc(m_full, 1)

            pe.wait_ge(m_out, 1)
            turn_tiles(0)
            pe.wait_ge(m_out, 1 + TT)
            pe.wait_ge(ld2[1], 16)
            for m_ in range(C):
                plain(work[m_][:], lambda c: wq2[:, c, m_ * P:(m_ + 1) * P],
                      lambda c: hT[:, c]).then_inc(m_full, 1)
            pe.wait_ge(m_out, 1 + TT + C)
            for t in range(TT):
                plain(yb[t][:, 0:P], lambda c: hT[:, c, t * P:(t + 1) * P],
                      lambda c: gT[:, c, t * P:(t + 1) * P]).then_inc(m_full, 1)
            for t in range(TT):
                pe.wait_ge(pre_done, 2 * (t + 1))
                pe.matmul(work[t][:], pre[:, t], hn[:, t], start=True, stop=True).then_inc(m_full, 1)
            turn_tiles(1)
            pe.wait_ge(ld2[2], 16)
            for t in range(TT):
                pe.wait_ge(m_out, 1 + TT + C + t + 1)
                last = plain(work[0][:, t * E:(t + 1) * E], lambda c: hT[:, c, t * P:(t + 1) * P],
                             lambda c: gw[:, c])
            last.then_inc(m_full, 1)
            pe.wait_ge(zeroed, 5)
            pe.wait_ge(chosen_done, 1)
            for t in range(TT):
                for u in range(t + 1):
                    last = pe.matmul(work[1][:, t * E:(t + 1) * E], (before if u == t else ones)[:], chosen[:, u],
                                     start=(u == 0), stop=(u == t))
            last.then_inc(m_full, 1)
            for t in range(TT):
                last = pe.matmul(yb[0][:, 0:E], ones[:], chosen[:, t],
                                 start=(t == 0), stop=(t == TT - 1))
            last.then_inc(m_full, 1)

            def gather(n):
                pe.wait_ge(pick_done, TT * (n + 1))
                for c in range(C):
                    dst = work[2 + c // 2][:, (c % 2) * SLOTS:(c % 2 + 1) * SLOTS]
                    for t in range(TT):
                        for i in range(2):
                            last = pe.matmul(dst, xn[i][:, t, c * P:(c + 1) * P], pick[:, t],
                                             start=(t == 0 and i == 0), stop=(t == TT - 1 and i == 1))
                    if c % 2:
                        last.then_inc(xg_full, 1)

            def places(n):
                pe.wait_ge(row_done, n + 1)
                pe.matmul(yb[2][:], ones_e[:], place_e[:], start=True, stop=True).then_inc(row_full, 1)

            def scatter(n):
                pe.wait_ge(put_done, ST * (n + 1))
                pe.wait_ge(y_lo, ST * (n + 1))
                for t in range(TT):
                    if t >= 2:
                        pe.wait_ge(y_out, TT * (n + 1) + t - 1)
                    for st in range(ST):
                        for i in range(2):
                            last = pe.matmul(yb[2 + t % 2][:], put[:, st, t * P:(t + 1) * P], ys[i][:, st],
                                             start=(st == 0 and i == 0), stop=(st == ST - 1 and i == 1))
                    last.then_inc(y_put, 1)

            def hidden(n, p, fresh=False):
                s = p % 2
                pe.wait_ge(w1_lo, NP * n + p + 1)
                if p == 0:
                    pe.wait_ge(xg_lo, 2 * (n + 1))
                for f in range(FC):
                    if f % 2 == 0 and not fresh:
                        pe.wait_ge(h_relu, FC * (NP * n + p) + f - 2)
                    last = products(work[f // 2][:, (f % 2) * SLOTS:(f % 2 + 1) * SLOTS],
                             lambda i, c: w1s[i][:, s, c, f * P:(f + 1) * P],
                             lambda i, c: xg[i][:, c])
                    if f % 2:
                        last.then_inc(h_full, 1)

            def second(n, p):
                s = p % 2
                pe.wait_ge(w2_lo, NP * n + p + 1)
                if p == 0:
                    if isinstance(n, int) and n == 0:
                        pe.wait_ge(y_out, TT)
                    else:
                        pe.wait_ge(y_lo, ST * n)
                for f in range(FC):
                    pe.wait_ge(h_lo, FC * (NP * n + p) + f + 1)
                    for st in range(ST):
                        for i, k in PASSES:
                            last = pe.matmul(yb[st][:], hs[i][:, s, f, st * P:(st + 1) * P], w2s[k][:, s, f],
                                             start=(p == 0 and f == 0 and (i, k) == (0, 0)),
                                             stop=(p == NP - 1 and f == FC - 1 and (i, k) == (1, 0)))
                last.then_inc(p2_used, 1)

            def biases():
                pe.wait_ge(cwT_done, 1)
                pe.wait_ge(ld2[5], 16)
                for t in range(TT):
                    pe.matmul(yb[t][:], cwT[:, t * P:(t + 1) * P], b2s[:], start=True, stop=True).then_inc(m_full, 1)

            def turn_rows():
                for t in range(TT):
                    last = pe.transpose(yb[2][0:E, t * P:(t + 1) * P], place[:, t, 0:E], ident[:])
                last.then_inc(m_full, 1)
                pe.wait_ge(cw_done, 1)
                for t in range(TT):
                    last = pe.transpose(yb[3][0:E, t * P:(t + 1) * P], cw[:, t], ident[:])
                last.then_inc(m_full, 1)

            def expert(n, first=False, last=False):
                for p in range(NP):
                    if p == 2 and not last:
                        gather(n + 1)
                    if p == 2:
                        places(n)
                    if p < NP - 1:
                        hidden(n, p + 1)
                    elif not last:
                        hidden(n + 1, 0)
                    if p == 0 and isinstance(n, int) and n == 0:
                        biases()
                    second(n, p)
                    if p == 0 and not first:
                        scatter(n - 1)

            def experts(ph):
                gather(E * ph)
                hidden(E * ph, 0, ph == 0)
                if ph == 0:
                    turn_rows()
                expert(E * ph, first=True)
                with pe.Fori(1, LASTE) as e:
                    expert(e + E * ph)
                expert(E * ph + LASTE, last=True)
                scatter(E * ph + LASTE)

            pe.wait_ge(x_lo, TT)
            experts(0)
            overflow(pe, experts)

        @block.vector
        def _(dve):
            steps = [0]

            def step(ins):
                ins.then_inc(chain, 1)
                steps[0] += 1

            def join():
                dve.wait_ge(chain, steps[0])

            def layer_norm(src, dst, signal, o):
                st = stat[:, 0:24].rearrange("p (t s) -> p t s", t=TT)
                mv = stat[:, 24:32].rearrange("p (t s) -> p t s", t=TT)
                for t in range(TT):
                    step(dve.bn_stats(st[:, t], src[:, t]))
                join()
                for t in range(TT):
                    step(dve.bn_aggr(mv[:, t], st[:, t]))
                join()
                v, root, y, z = (stat[:, c:c + TT] for c in (40, 44, 32, 48))
                dve.tensor_scalar(v, mv[:, :, 1], EPS, None, ALU.add).then_inc(var_done, 1)
                dve.wait_ge(root_done, o)
                for ins in (lambda: dve.reciprocal(y, root),
                            lambda: dve.tensor_tensor(z, y, y, ALU.mult),
                            lambda: dve.tensor_tensor(z, z, v, ALU.mult),
                            lambda: dve.tensor_scalar(z, z, -0.5, 1.5, ALU.mult, ALU.add),
                            lambda: dve.tensor_tensor(y, y, z, ALU.mult)):
                    step(ins())
                    join()
                for t in range(TT):
                    dve.tensor_scalar(dst[:, t], src[:, t], mv[:, t, 0:1], stat[:, 32 + t:33 + t],
                                      ALU.subtract, ALU.mult).then_inc(signal, 1)

            dve.wait_ge(ld_x, 16)
            layer_norm(xin, xin, ln1, 1)
            step(dve.memset(negmask[:, LK:LKP], LOWEST))

            def convert_mask(b):
                dve.wait_ge(ld_mask, 16 * (b + 1))
                dve.tensor_scalar(negmask[:, 0:LK], pr[:, 0, 0:LK].bitcast(I32), 0.0, LOWEST,
                                  ALU.is_gt, ALU.mult).then_inc(mask_done, 1)

            join()
            convert_mask(0)
            for i, w in enumerate((kw, vw)):
                dve.wait_ge(w_hi, i + 1)
                dve.tensor_tensor(w[1][:], wraw[:], w[0][:].bitcast(F32), ALU.subtract).then_inc(w_lo, 1)

            def key_lo(h, j, bank):
                k, m = j // 2, j % 2
                sl = slice(k * KC, (k + 1) * KC)
                col = C + 2 * h + m
                dve.scalar_tensor_tensor(out=kk[1][:, m, sl], in0=work[bank][:, 0:KC],
                                         scalar=biasT[:, col:col + 1], in1=kk[0][:, m, sl].bitcast(F32),
                                         op0=ALU.add, op1=ALU.subtract).then_inc(w_free, 1)

            def query_blocks(b, h):
                def parts(a):
                    rows = slice(HD * a, HD * (a + 1))
                    cols = slice((a % 2) * S, (a % 2 + 1) * S)
                    tok = slice(b * S, (b + 1) * S) if isinstance(b, int) else bass.ds(b * S, S)
                    return qT[rows, 2 * h:2 * h + 2, tok], [q[rows, :, a // 2, cols] for q in qbd]

                for a in range(HPC):
                    src, (hi, lo) = parts(a)
                    dve.tensor_copy(hi, src).then_inc(qbd_done, 1)
                own(dve, qbd_done, (2 * b + h) * 2 * HPC + HPC)
                for a in range(HPC):
                    src, (hi, lo) = parts(a)
                    dve.tensor_tensor(lo, src, hi.bitcast(F32), ALU.subtract).then_inc(qbd_done, 1)

            def item(b, last, step):
                kind, a, k = step
                i = ITEMS[last].index(step)
                bank = work[i % 4]
                if kind in "kv":
                    dve.wait_ge(kv_hi, NKV * b + FIRST_K + KV[last].index(step) + 1)
                if kind == "k":
                    key_lo(a, k, i % 4)
                elif kind == "v":
                    n = min(2, KT - 2 * k)
                    dve.tensor_tensor(vv[1][:, 2 * k:2 * k + n, :],
                                      bank[:, 0:n * 2 * P].rearrange("p (n d) -> p n d", n=n),
                                      vv[0][:, 2 * k:2 * k + n, :].bitcast(F32), ALU.subtract).then_inc(w_free, 1)
                elif kind == "s":
                    own(dve, w_full, count(b, last, step))
                    sl = slice(k * KC, (k + 1) * KC)
                    dve.tensor_tensor_reduce(pr[:, a % 4, sl], bank[:, 0:KC], negmask[:, sl], SCALE, LOWEST,
                                             ALU.add, ALU.max, smx[:, a, k:k + 1]).then_inc(w_free, 1)
                    if k == NKC - 1:
                        dve.wait_ge(w_free, count(b, last, step))
                        dve.tensor_reduce(nmx[:, a:a + 1], smx[:, a], AX.X, ALU.max,
                                          negate=True).then_inc(raw_nmx, 1)
                        own(dve, raw_nmx, 8 * b + a + 1)
                        dve.tensor_scalar(nmx[:, a:a + 1], nmx[:, a:a + 1], 1024.0, 1 / 1024.0,
                                          ALU.mult, ALU.mult).then_inc(nmx_done, 1)
                else:
                    dve.wait_ge(w_full, count(b, last, step))
                    dve.tensor_copy(recip[:, a % 2], bank[:, 0:2 * P]).then_inc(w_free, 1)

            def reciprocal(b, r):
                dve.wait_ge(exp_done, 8 * b + r + 1)
                dve.reciprocal(rinv[:, r:r + 1], rsum[:, r:r + 1]).then_inc(rinv_done, 1)
                dve.wait_ge(rinv_done, 8 * b + r + 1)
                dve.tensor_scalar(diag[:, r % 4], ident[:], rinv[:, r:r + 1], None, ALU.mult).then_inc(diag_done, 1)

            def pt_item(b, j):
                dve.wait_ge(pt_hi, NPT * b + j + 1)
                n = min(2, KT - 2 * (j % TPH))
                dve.tensor_tensor(pt[1][:, j % PTD, 0:n],
                                  ptp[j % PTD][:, 0:n * 2 * P].rearrange("p (n d) -> p n d", n=n),
                                  pt[0][:, j % PTD, 0:n].bitcast(F32), ALU.subtract).then_inc(pt_lo, 1)

            def group_out(b, last, g):
                dve.wait_ge(pt_used, NPT * b + TPH * (g + 1) + PTD)
                dve.wait_ge(w_free, count(b, last, ("r", g, 0)))
                for a in range(HPC):
                    rows, cols = slice(HD * a, HD * (a + 1)), slice(S * a, S * (a + 1))
                    tok = slice(b * S, (b + 1) * S) if isinstance(b, int) else bass.ds(b * S, S)
                    ins = dve.tensor_tensor(qT[rows, g, tok], pv[rows, cols], recip[rows, g % 2, cols], ALU.mult)
                ins.then_inc(pv_free, 1)

            def body(b, last=False):
                for step in STEPS[last]:
                    kind, a, j = step
                    if kind == "w":
                        lo, hi = (0, TPH + 2) if a % 2 == 0 else (TPH + 2, 2 * TPH)
                        for i in range(lo, hi):
                            pt_item(b, 2 * TPH * (a // 2) + i)
                        group_out(b, last, a)
                        continue
                    if kind == "r" and a % 2 == 0:
                        for r in range(2 * a, 2 * a + 4):
                            reciprocal(b, r)
                    item(b, last, step)
                    if step == ("s", 3, NKC - 1):
                        query_blocks(b, 1)
                    if step == ("s", 7, NKC - 1) and not last:
                        query_blocks(b + 1, 0)
                if not last:
                    convert_mask(b + 1)

            for j in range(FIRST_K):
                dve.wait_ge(kv_hi, j + 1)
                key_lo(0, j, j % 4)
            dve.wait_ge(q_done, C)
            dve.wait_ge(consts, 5)
            query_blocks(0, 0)
            dve.sem_inc(pt_lo, PTD)
            dve.sem_inc(pv_free, 1)
            dve.wait_ge(mask_done, 1)
            with dve.Fori(0, LASTB) as b:
                body(b)
                dve.wait_ge(mask_done, b + 2)
            body(LASTB, True)
            dve.wait_ge(pv_free, 4 * B + 1)
            dve.sem_inc(att_over, 1)

            dve.wait_ge(ld2[0], 16)
            for t in range(TT):
                dve.wait_ge(m_full, t + 1)
                step(dve.tensor_tensor(xs[:, t], xs[:, t], work[t][:], ALU.add))
            join()
            layer_norm(xs, hn, ln2, 2)
            dve.wait_ge(zeroed, 5)
            for t in range(TT):
                dve.wait_ge(m_full, 14 + t)
                for a in range(2):
                    r = slice(S * a, S * (a + 1))
                    dve.tensor_copy(pre[r, t, r], yb[t][r, r]).then_inc(pre_done, 1)
            for t in range(TT):
                dve.wait_ge(m_full, 18 + t)
                step(dve.tensor_tensor(xs[:, t], xs[:, t], work[t][:], ALU.add))
            join()
            layer_norm(xs, hn, ln2, 3)
            dve.wait_ge(ld2[3], 16)
            dve.wait_ge(m_full, 26)
            dve.tensor_copy(ones_e[:], ones[0:E, :]).then_inc(placeT_done, 1)
            step(dve.tensor_tensor(logit[:], work[0][:, 0:TT * E].rearrange("p (t e) -> p t e", t=TT), gb[:], ALU.add))
            join()
            for t in range(TT):
                step(dve.max(top8[:, t], logit[:, t]))
            join()
            for t in range(TT):
                step(dve.max_index(idx8[:, t], top8[:, t], logit[:, t]))
            dve.tensor_tensor(wts[:, 0], top8[:, :, 1], top8[:, :, 0], ALU.subtract).then_inc(gate_diff, 1)
            join()
            step(dve.tensor_copy(idxf[:], idx8[:]))
            join()
            for k in range(2):
                step(dve.tensor_tensor(best[:, k], iota_e[:], idxf[:, :, k:k + 1].broadcast_to([P, TT, E]),
                                       ALU.is_equal))
            join()
            dve.tensor_tensor(chosen[:], best[:, 0], best[:, 1], ALU.add).then_inc(chosen_done, 1)
            dve.wait_ge(m_full, 27)
            dve.wait_ge(chosen_done, 1)
            dve.scalar_tensor_tensor(out=place[:, :, 0:E], in0=work[1][:, 0:TT * E].rearrange("p (t e) -> p t e", t=TT),
                                     scalar=1.0, in1=chosen[:], op0=ALU.add, op1=ALU.mult).then_inc(place_done, 1)
            dve.wait_ge(place_done, 1)

            def picks(n):
                for t in range(TT):
                    col = place[:, t, n:n + 1] if isinstance(n, int) else place[:, t, bass.ds(n, 1)]
                    dve.tensor_scalar(pick[:, t], iota_s[:], col, None, ALU.is_equal).then_inc(pick_done, 1)

            def gathered(n):
                for i in range(2):
                    dve.wait_ge(xg_hi, 2 * n + i + 1)
                    dve.tensor_tensor(xg[1][:, 2 * i:2 * i + 2], work[2 + i][:].rearrange("p (c n) -> p c n", c=2),
                                      xg[0][:, 2 * i:2 * i + 2].bitcast(F32), ALU.subtract).then_inc(xg_lo, 1)

            def row(n, e):
                mine = ident[0:E, e:e + 1] if isinstance(e, int) else ident[0:E, bass.ds(e, 1)]
                dve.tensor_scalar(place_e[:], placeT[:], mine, None, ALU.mult).then_inc(row_done, 1)

            def puts(ph, n):
                dve.wait_ge(row_full, n + 1)
                for st in range(ST):
                    dve.tensor_scalar(put[:, st], yb[2][:], slot_id[:, ph, st:st + 1], None,
                                      ALU.is_equal).then_inc(put_done, 1)

            def outputs(n):
                for i in range(ST):
                    dve.wait_ge(y_hi, ST * n + i + 1)
                    dve.tensor_tensor(ys[1][:, i], yb[i][:], ys[0][:, i].bitcast(F32), ALU.subtract).then_inc(y_lo, 1)

            def add_outputs(n, e):
                dve.wait_ge(y_out, TT * (n + 1))
                for t in range(TT):
                    dve.wait_ge(y_put, TT * n + t + 1)
                    col = cw[:, t, e:e + 1] if isinstance(e, int) else cw[:, t, bass.ds(e, 1)]
                    dve.scalar_tensor_tensor(out=xs[:, t], in0=yb[2 + t % 2][:], scalar=col, in1=xs[:, t],
                                             op0=ALU.mult, op1=ALU.add).then_inc(y_out, 1)

            def w1_part(n, p):
                s = p % 2
                dve.wait_ge(w1_hi, NP * n + p + 1)
                dve.tensor_tensor(w1s[1][:, s], w1raw[:, s], w1s[0][:, s].bitcast(F32),
                                  ALU.subtract).then_inc(w1_lo, 1)

            def w2_part(n, p):
                s = p % 2
                dve.wait_ge(w2_hi, NP * n + p + 1)
                dve.tensor_tensor(w2s[1][:, s], w2raw[:, s], w2s[0][:, s].bitcast(F32),
                                  ALU.subtract).then_inc(w2_lo, 1)

            def biases():
                for t in range(TT):
                    dve.wait_ge(m_full, 31 + t)
                    dve.tensor_tensor(xs[:, t], xs[:, t], yb[t][:], ALU.add).then_inc(y_out, 1)

            def expert(ph, e, first=False, last=False):
                n = e + E * ph
                for p in range(NP):
                    if p < NP - 1:
                        w1_part(n, p + 1)
                    elif not last:
                        w1_part(n + 1, 0)
                    w2_part(n, p)
                    for f in range(FC):
                        c = FC * (NP * n + p) + f
                        dve.wait_ge(h_hi, c + 1)
                        dve.tensor_tensor(hs[1][:, p % 2, f], hf[:, f], hs[0][:, p % 2, f].bitcast(F32),
                                          ALU.subtract).then_inc(h_lo, 1)
                    if p == 0 and not first:
                        outputs(n - 1)
                        add_outputs(n - 1, e - 1)
                    if p == 0 and isinstance(n, int) and n == 0:
                        biases()
                    if p == 1:
                        row(n, e)
                        if not last:
                            picks(n + 1)
                    if p == 2:
                        puts(ph, n)
                if not last:
                    gathered(n + 1)

            def experts(ph):
                if ph:
                    w1_part(E * ph, 0)
                    picks(E * ph)
                    gathered(E * ph)
                expert(ph, 0, first=True)
                with dve.Fori(1, LASTE) as e:
                    expert(ph, e)
                expert(ph, LASTE, last=True)
                outputs(E * ph + LASTE)
                add_outputs(E * ph + LASTE, LASTE)
                dve.wait_ge(y_out, TT * (E * (ph + 1) + 1))

            w1_part(0, 0)
            picks(0)
            dve.wait_ge(gate_exp, 1)
            step(dve.tensor_scalar(wts[:, 0], wts[:, 1], 1.0, None, ALU.add))
            step(dve.tensor_scalar(place[:, :, E:2 * E], place[:, :, 0:E], -float(SLOTS), None, ALU.add))
            join()
            step(dve.reciprocal(wts[:, 2], wts[:, 0]))
            join()
            step(dve.tensor_tensor(wts[:, 3], wts[:, 1], wts[:, 2], ALU.mult))
            gathered(0)
            dve.wait_ge(m_full, 28)
            step(dve.tensor_reduce(total[:, 0:1], yb[0][:, 0:E], AX.X, ALU.max))
            join()
            for k, dst in ((0, cw), (1, cw2)):
                step(dve.tensor_tensor(dst[:], best[:, k], wts[:, 2 + k].rearrange("p (t o) -> p t o", o=1)
                                       .broadcast_to([P, TT, E]), ALU.mult))
            join()
            dve.tensor_tensor(cw[:], cw[:], cw2[:], ALU.add).then_inc(cw_done, 1)
            dve.tensor_scalar(crowded[:], total[:, 0:1], float(SLOTS), None, ALU.is_gt).then_inc(flag_done, 1)
            dve.wait_ge(m_full, 29)
            step(dve.tensor_copy(placeT[:], yb[2][0:E, :]))
            dve.wait_ge(m_full, 30)
            dve.tensor_copy(cwT[:], yb[3][0:E, :]).then_inc(cwT_done, 1)
            join()
            experts(0)
            overflow(dve, experts)
            dve.sem_inc(result_done, 1)


def kernel(**inputs):
    import numpy as np
    import concourse.bacc as bacc
    from concourse.bass_utils import run_bass_kernel_spmd

    def a(name):
        return np.asarray(inputs[name])

    ctxT = np.zeros((B, D, KP), np.float32)
    ctxT[:, :, :LK] = a("ctx_1024").transpose(0, 2, 1)
    arrays = {
        "x": a("x").reshape(T, D), "ctxT": ctxT, "mask": a("mask_BxS2_ik0"),
        "qwT": a("L0_xattn_q_w").T, "kwT": a("L0_xattn_k_w").T, "vwT": a("L0_xattn_v_w").T,
        "wqT": a("L0_attn_W_q").T,
        "bias3": np.concatenate([a("L0_xattn_q_b"), a("L0_xattn_k_b"), a("L0_xattn_v_b")]).reshape(3 * C, P),
        "gate_w": a("L0_ffn_gate_w"), "gate_b": np.tile(a("L0_ffn_gate_b"), TT).reshape(1, TT * E),
        "w1": a("L0_ffn_w1"), "b1": a("L0_ffn_b1"), "w2": a("L0_ffn_w2"), "b2": a("L0_ffn_b2"),
    }
    arrays = {f"in_{n}": np.ascontiguousarray(v) for n, v in arrays.items()}
    nc = bacc.Bacc("TRN2", target_bir_lowering=False, num_devices=1)
    args = [nc.dram_tensor(n, v.shape, mybir.dt.from_np(v.dtype), kind="ExternalInput").ap()
            for n, v in arrays.items()]
    out = nc.dram_tensor("out", (T, D), F32, kind="ExternalOutput").ap()
    layer(nc, *args, out)
    r = run_bass_kernel_spmd(nc, [arrays], core_ids=[0])
    return r.results[0]["out"].reshape(B, S, D)
```

```python
from contextlib import ExitStack

import concourse.bass as bass
from concourse import mybir

ALU = mybir.AluOpType
ACT = mybir.ActivationFunctionType
AX = mybir.AxisListType
F32 = mybir.dt.float32
F32R = mybir.dt.float32r
BF16 = mybir.dt.bfloat16
I32 = mybir.dt.int32
U32 = mybir.dt.uint32

P = 128
BANK = 512
B, S, D = 8, 64, 512
T = B * S
TT = T // P
C = D // P
LK = 1601
HD = 32
HPC = P // HD
KT = -(-LK // P)
KP = KT * P
KC = 402
NKC = 4
LKP = KC * NKC
CC = KP // NKC
E, F = 8, 2048
NP = F // 512
FC = 4
HB = FC // 2
SLOTS = 256
ST = SLOTS // P
BLOCKS = T // SLOTS
SCALE = float(HD) ** -0.5
EPS = 1e-5
LOWEST = -3.0e38


def steps_of(last):
    steps = []
    for h in range(2):
        v = [("v", h, j) for j in range((KT + 1) // 2)]
        k = [] if h and last else [("k", 1 - h, j) for j in range(2 * NKC)]
        s = [[("s", 4 * h + r, j) for j in range(NKC)] for r in range(4)]
        e = [("e", 4 * h + r, 0) for r in range(4)]
        d = [("d", 2 * h, 0)]
        r = [("r", 2 * h, 0), ("r", 2 * h + 1, 0)]
        t, w = [("t", 2 * h, 0)], [("w", 2 * h, 0), ("w", 2 * h + 1, 0)]
        steps += v[:3]
        if k:
            for i in range(4):
                steps += s[i] + v[3 + i:4 + i] + e[i:i + 1]
            steps += k[:2] + d + k[2:4] + r + k[4:6] + t + k[6:7] + w[:1] + k[7:] + w[1:]
        else:
            steps += s[0] + v[3:4] + e[:1] + s[1] + e[1:2] + s[2] + e[2:3] + s[3] + v[4:5] + e[3:]
            steps += d + v[5:6] + r[:1] + v[6:] + t + w[:1] + r[1:] + w[1:]
    return steps


STEPS = [steps_of(False), steps_of(True)]
ITEMS = [[s for s in steps if s[0] in "vskr"] for steps in STEPS]
KV = [[s for s in items if s[0] in "kv"] for items in ITEMS]
NW = len(ITEMS[0])
NKV = len(KV[0])
FIRST_K = 2 * NKC
NPT = 2 * (KT + 1)
PTD = 3
TPH = KT // 2 + 1


def turns(step):
    if step[0] not in "tw":
        return range(0)
    g, base = step[1], 2 * TPH * (step[1] // 2)
    if step[0] == "t":
        return range(base, base + 2)
    return range(base + 2, base + TPH + 2) if g % 2 == 0 else range(base + TPH + 2, base + 2 * TPH)


def count(b, last, step):
    return NW * b + FIRST_K + ITEMS[last].index(step) + 1


def spare(step):
    return step[0] == "v" and step[2] >= 3


RING = [[s for s in items if not spare(s)] for items in ITEMS]


def bank_of(last, step):
    return (step[2] - 3) % PTD if spare(step) else RING[last].index(step) % 4


def before_bank(b, last, step):
    q = RING[last].index(step)
    if q >= 4:
        return count(b, last, RING[last][q - 4])
    other = max(m for m in range(len(RING[0])) if m % 4 == q)
    return NW * b + FIRST_K + max(ITEMS[0].index(RING[0][other]) + 1 - NW, q - 3)


def pt_before(j):
    last = j - PTD if j >= PTD else max(m for m in range(NPT) if m % PTD == j) - NPT
    return last + 1 + PTD


def layer(nc, x, ctxT, mask, qwT, kwT, vwT, wqT, bias3, gate_w, gate_b, w1, b1, w2, b2, out):
    with ExitStack() as top:
        def sem(name):
            return top.enter_context(nc.semaphore(name))

        def sb(stack, name, shape, dt):
            return stack.enter_context(nc.sbuf_tensor(name, shape, dt))

        work = [top.enter_context(nc.psum_tensor(f"work{i}", [P, BANK], F32)) for i in range(4)]
        ptp = [top.enter_context(nc.psum_tensor(f"ptp{i}", [P, BANK], F32)) for i in range(3)]
        pv = top.enter_context(nc.psum_tensor("pv", [P, BANK], F32))

        ident = sb(top, "ident", [P, P], F32)
        ones = sb(top, "ones", [P, P], F32)
        qT = sb(top, "qT", [P, C, T], F32)
        biasT = sb(top, "biasT", [P, 3 * C], F32)
        stat = sb(top, "stat", [P, 64], F32)

        with ExitStack() as m:
            kw = [sb(m, f"kw_{n}", [P, C, D], F32R) for n in ("hi", "lo")]
            vw = [sb(m, f"vw_{n}", [P, C, D], F32R) for n in ("hi", "lo")]
            cx = [sb(m, f"cx_{n}", [P, C, KP], F32R) for n in ("hi", "lo")]
            kk = [sb(m, f"kk_{n}", [P, 2, LKP], F32R) for n in ("hi", "lo")]
            pr = sb(m, "pr", [P, 4, KP], F32)
            negmask = sb(m, "negmask", [P, LKP], BF16)
            raw = sb(m, "raw", [P, 2, C, CC], F32)
            qbd = [sb(m, f"qbd_{n}", [P, 2, 2, P], F32R) for n in ("hi", "lo")]
            diag = sb(m, "diag", [P, 4, P], F32)
            recip = sb(m, "recip", [P, 2, 2 * P], F32)
            smx = sb(m, "smx", [P, 8, NKC], F32)
            nmx = sb(m, "nmx", [P, 8], F32)
            rsum = sb(m, "rsum", [P, 8], F32)
            rinv = sb(m, "rinv", [P, 8], F32)
            with ExitStack() as m2:
                vv = [sb(m2, f"vv_{n}", [P, KT, 2 * P], F32R) for n in ("hi", "lo")]
                pt = [sb(m2, f"pt_{n}", [P, PTD, 2, 2 * P], F32R) for n in ("hi", "lo")]
            xin = sb(m, "xin", [P, TT, D], F32)
            xnT = sb(m, "xnT", [P, C, T], F32)
            qwraw = sb(m, "qwraw", [P, C, D], F32)
            kwraw = sb(m, "kwraw", [P, C, D], F32)
            brow = sb(m, "brow", [3 * C, P], F32)

        with ExitStack() as m:
            xs = sb(m, "xs", [P, TT, D], F32)
            wq2 = sb(m, "wq2", [P, C, D], F32)
            gw = sb(m, "gw", [P, C, E], F32)
            gb = sb(m, "gb", [P, TT, E], F32)
            b1r = sb(m, "b1r", [P, P], F32)
            b2s = sb(m, "b2s", [E, D], F32)
            w1raw = sb(m, "w1raw", [P, 2, C, 512], F32)
            w2raw = sb(m, "w2raw", [P, 2, FC, D], F32)
            hn = sb(m, "hn", [P, TT, D], F32)
            with ExitStack() as m2:
                hT = sb(m2, "hT", [P, C, T], F32)
            ys = [sb(m, f"y_{n}", [P, ST, D], F32R) for n in ("hi", "lo")]
            b1T = sb(m, "b1T", [P, P], F32)
            logit = sb(m, "logit", [P, TT, E], F32)
            top8 = sb(m, "top8", [P, TT, 8], F32)
            idx8 = sb(m, "idx8", [P, TT, 8], U32)
            idxf = sb(m, "idxf", [P, TT, 8], F32)
            iota_e = sb(m, "iota_e", [P, TT, E], F32)
            iota_s = sb(m, "iota_s", [P, SLOTS], F32)
            slot_id = sb(m, "slot_id", [P, BLOCKS, ST], F32)
            ones16 = sb(m, "ones16", [P, P], BF16)
            before = sb(m, "before", [P, P], BF16)
            wts = sb(m, "wts", [P, 4, TT], F32)
            best = sb(m, "best", [P, 2, TT, E], F32)
            chosen = sb(m, "chosen", [P, TT, E], BF16)
            place = sb(m, "place", [P, TT, BLOCKS * E], F32)
            total = sb(m, "total", [P, 4], F32)
            crowded = sb(m, "crowded", [P, 1], I32)
            cw = sb(m, "cw", [P, TT, E], F32)
            cw2 = sb(m, "cw2", [P, TT, E], F32)
            cwT = sb(m, "cwT", [E, T], F32)
            placeT = sb(m, "placeT", [E, T], F32)
            place_e = sb(m, "place_e", [E, T], F32R)
            ones_e = sb(m, "ones_e", [E, P], F32R)
            xn = [sb(m, f"xn_{n}", [P, TT, D], F32R) for n in ("hi", "lo")]
            w1s = [sb(m, f"w1_{n}", [P, 2, C, 512], F32R) for n in ("hi", "lo")]
            hf = sb(m, "hf", [P, FC, SLOTS], F32)
            w2s = [sb(m, f"w2_{n}", [P, 2, FC, D], F32R) for n in ("hi", "lo")]
            with ExitStack() as m2:
                gT = sb(m2, "gT", [P, C, T], F32)
                pre = sb(m2, "pre", [P, TT, P], F32)
            hs = [sb(m, f"h_{n}", [P, 2, FC, SLOTS], F32R) for n in ("hi", "lo")]
            xg = [sb(m, f"xg_{n}", [P, C, SLOTS], F32R) for n in ("hi", "lo")]
            pick = sb(m, "pick", [P, TT, SLOTS], F32R)
            put = sb(m, "put", [P, ST, T], F32R)

        vwraw = pr[:, 1:3, 0:D * C // 2].rearrange("p a (b n) -> p a b n", n=D)

        ld_x, ld_b = sem("x_loaded"), sem("biases_loaded")
        ld_qw, ld_vw = sem("q_weight_loaded"), sem("v_weight_loaded")
        ld_kw = [sem(f"k_weight_half_loaded{h}") for h in range(2)]
        ld_raw = [sem(f"context_chunk_loaded{i}") for i in range(2)]
        ld_mask = sem("mask_loaded")
        consts = sem("constants_ready")
        chain = sem("vector_step")
        ln1 = sem("x_normalised")
        var_done, root_done = sem("variance_ready"), sem("root_ready")
        t_full = sem("pre_psum_full")
        t_out = sem("pre_psum_drained")
        w_hi, w_lo = sem("weight_hi"), sem("weight_lo")
        c_hi, c_lo = sem("context_hi"), sem("context_lo")
        q_done = sem("queries_ready")
        qbd_done = sem("query_blocks_ready")
        w_full = sem("work_bank_full")
        kv_hi = sem("keys_values_hi")
        w_free = sem("work_bank_drained")
        raw_nmx = sem("raw_row_maximum")
        nmx_done = sem("row_maximum_ready")
        exp_done = sem("row_exponentials_ready")
        rinv_done = sem("row_reciprocal")
        diag_done = sem("reciprocal_diagonal_ready")
        pt_full, pt_hi, pt_lo = sem("probabilities_transposed"), sem("probabilities_hi"), sem("probabilities_lo")
        pt_used = sem("probabilities_used")
        pv_free = sem("weighted_values_drained")
        mask_done = sem("mask_ready")
        att_over = sem("attention_over")
        ld2 = [sem(f"late_load{i}") for i in range(6)]
        zeroed = sem("late_constants_ready")
        ob_done = sem("attention_bias_added")
        m_full, m_out = sem("mid_psum_full"), sem("mid_psum_copied")
        x_add, ln2 = sem("residual_added"), sem("residual_normalised")
        pre_done = sem("self_scores_ready")
        gate_diff, gate_exp = sem("gate_difference"), sem("gate_exponential")
        x_hi, x_lo = sem("moe_input_hi"), sem("moe_input_lo")
        chosen_done, place_done = sem("choice_ready"), sem("places_ready")
        placeT_done, flag_done = sem("places_transposed"), sem("crowded_ready")
        pick_done, xg_full, xg_hi, xg_lo = sem("pick_ready"), sem("gathered"), sem("gathered_hi"), sem("gathered_lo")
        row_done, row_full, put_done = sem("expert_places_ready"), sem("places_broadcast"), sem("put_ready")
        y_hi, y_lo, y_put = sem("output_hi"), sem("output_lo"), sem("output_scattered")
        result_done = sem("result_ready")
        cw_done, cwT_done = sem("expert_weights_ready"), sem("expert_weights_transposed")
        ld_w1 = [sem(f"w1_loaded{i}") for i in range(2)]
        ld_w2 = [sem(f"w2_loaded{i}") for i in range(2)]
        w1_hi, w1_lo, w2_hi, w2_lo = sem("w1_hi"), sem("w1_lo"), sem("w2_hi"), sem("w2_lo")
        h_full, h_relu, h_hi, h_lo = sem("hidden_full"), sem("hidden_relu"), sem("hidden_hi"), sem("hidden_lo")
        p2_used = sem("w2_piece_used")
        y_out = sem("expert_output_added")
        stored = sem("output_stored")

        LASTB, LASTE = B - 1, E - 1
        yb = ptp + [pv]
        block = top.enter_context(nc.Block())

        def own(eng, sem, value):
            eng.wait_ge(sem, value)
            if not isinstance(value, int):
                eng.nop(nofuse=True)

        def overflow(eng, experts):
            eng.wait_ge(flag_done, 1)
            with eng.If(eng.value_load(crowded[0:1, 0:1], min_val=0, max_val=1) > 0):
                experts(1)
                eng.nop(nofuse=True)

        @block.sync
        def _(sp):
            def load_chunk(b, k, first=False):
                if not first:
                    own(sp, c_lo, NKC * b + k - 1)
                src = ctxT[b:b + 1] if isinstance(b, int) else ctxT[bass.ds(b, 1)]
                sp.dma_start(raw[:, k % 2], src[:, :, k * CC:(k + 1) * CC].rearrange(
                    "o (c p) n -> p (o c) n", p=P)).then_inc(ld_raw[k % 2], 16)

            def load_mask(b):
                src = mask[b:b + 1, :] if isinstance(b, int) else mask[bass.ds(b, 1), :]
                sp.dma_start(pr[:, 0, 0:LK].bitcast(I32), src.broadcast_to([P, LK])).then_inc(ld_mask, 16)

            sp.dma_start(brow[:], bias3).then_inc(ld_b, 16)
            def load_kw(h):
                cols = slice(h * D // 2, (h + 1) * D // 2)
                sp.dma_start(kwraw[:, :, cols], kwT[:, cols].rearrange("(c p) n -> p c n", p=P)).then_inc(ld_kw[h], 16)

            load_kw(0)
            load_chunk(0, 0, True)
            load_chunk(0, 1, True)
            sp.dma_start(xin[:], x.rearrange("(t p) d -> p t d", p=P)).then_inc(ld_x, 16)
            load_chunk(0, 2)
            load_kw(1)
            sp.dma_start(qwraw[:], qwT.rearrange("(c p) n -> p c n", p=P)).then_inc(ld_qw, 16)
            load_chunk(0, 3)
            for a in range(2):
                sp.dma_start(vwraw[:, a], vwT[a * D // 2:(a + 1) * D // 2, :].rearrange("(b p) n -> p b n", p=P)
                             ).then_inc(ld_vw, 16)
            load_mask(0)

            with sp.Fori(0, LASTB) as b:
                for k in range(NKC):
                    load_chunk(b + 1, k)
                own(sp, pt_full, NPT * b + 3 * TPH)
                load_mask(b + 1)

            sp.wait_ge(w_free, count(LASTB, 1, ("v", 1, TPH - 1)))
            sp.dma_start(xs[:], x.rearrange("(t p) d -> p t d", p=P)).then_inc(ld2[0], 16)
            sp.dma_start(b1r[:], b1.rearrange("e (k j) -> (e k) j", j=P)).then_inc(ld2[4], 16)
            sp.dma_start(wq2[:], wqT.rearrange("(c p) n -> p c n", p=P)).then_inc(ld2[1], 16)
            sp.dma_start(gw[:], gate_w.rearrange("(c p) n -> p c n", p=P)).then_inc(ld2[2], 16)
            sp.dma_start(gb[:], gate_b.broadcast_to([P, TT * E])).then_inc(ld2[3], 16)
            sp.dma_start(b2s[:], b2).then_inc(ld2[5], 16)

            def load_w1(ph, e, p, first=False):
                s, n = p % 2, e + E * ph
                if not first:
                    own(sp, w1_lo, NP * n + p - 1)
                src = w1[e:e + 1] if isinstance(e, int) else w1[bass.ds(e, 1)]
                sp.dma_start(w1raw[:, s], src[:, :, p * 512:(p + 1) * 512].rearrange(
                    "o (c p) n -> p (o c) n", p=P)).then_inc(ld_w1[s], 16)

            def load_w2(ph, e, p, first=False):
                s, n = p % 2, e + E * ph
                if not first:
                    own(sp, w2_lo, NP * n + p - 1)
                src = w2[e:e + 1] if isinstance(e, int) else w2[bass.ds(e, 1)]
                sp.dma_start(w2raw[:, s], src[:, p * 512:(p + 1) * 512, :].rearrange(
                    "o (c p) n -> p (o c) n", p=P)).then_inc(ld_w2[s], 16)

            def expert(ph, e, fresh=False, last=False):
                for p in range(NP):
                    if p < NP - 1:
                        load_w1(ph, e, p + 1, fresh and p == 0)
                    elif not last:
                        load_w1(ph, e + 1, 0)
                    load_w2(ph, e, p, fresh and p < 2)

            def experts(ph):
                load_w1(ph, 0, 0, ph == 0)
                expert(ph, 0, ph == 0)
                with sp.Fori(1, LASTE) as e:
                    expert(ph, e)
                expert(ph, LASTE, last=True)

            experts(0)
            overflow(sp, experts)
            sp.wait_ge(result_done, 1)
            sp.dma_start(out.rearrange("(t p) d -> p t d", p=P), xs[:]).then_inc(stored, 16)
            sp.wait_ge(stored, 16)

        @block.gpsimd
        def _(pool):
            pool.memset(ident[:], 0.0).then_inc(consts, 1)
            pool.memset(ones[:], 1.0).then_inc(consts, 1)
            pool.wait_ge(consts, 2)
            pool.affine_select(out=ident[:], in_=ident[:], compare_op=ALU.not_equal, fill=1.0, base=0,
                               pattern=[[-1, P]], channel_multiplier=1).then_inc(consts, 1)
            for q in qbd:
                pool.memset(q[:].bitcast(F32), 0.0).then_inc(consts, 1)
            pool.memset(pr[:, :, LKP:KP], 0.0).then_inc(consts, 1)
            pool.wait_ge(consts, 6)

            def ctx_lo(b, k):
                own(pool, c_hi, NKC * b + k + 1)
                sl = slice(k * CC, (k + 1) * CC)
                pool.tensor_tensor(cx[1][:, :, sl], raw[:, k % 2], cx[0][:, :, sl].bitcast(F32),
                                   ALU.subtract).then_inc(c_lo, 1)

            pool.wait_ge(c_lo, 1)
            for k in range(1, NKC):
                ctx_lo(0, k)
            with pool.Fori(1, B) as b:
                for k in range(NKC):
                    ctx_lo(b, k)
            pool.wait_ge(c_lo, NKC * B)
            pool.sem_inc(att_over, 1)

            pool.wait_ge(att_over, 4)
            pool.memset(pre[:], 0.0).then_inc(zeroed, 1)
            pool.iota(iota_e[:], pattern=[[0, TT], [1, E]], base=0, channel_multiplier=0,
                      allow_small_or_imprecise_dtypes=True).then_inc(zeroed, 1)
            pool.iota(iota_s[:], pattern=[[1, SLOTS]], base=1, channel_multiplier=0,
                      allow_small_or_imprecise_dtypes=True).then_inc(zeroed, 1)
            pool.iota(slot_id[:], pattern=[[SLOTS, BLOCKS], [P, ST]], base=1, channel_multiplier=1,
                      allow_small_or_imprecise_dtypes=True).then_inc(zeroed, 1)
            pool.memset(ones16[:], 1.0).then_inc(zeroed, 1)
            pool.wait_ge(zeroed, 5)
            pool.affine_select(out=before[:], in_=ones16[:], compare_op=ALU.is_gt, fill=0.0, base=0,
                               pattern=[[1, P]], channel_multiplier=-1).then_inc(zeroed, 1)
            for t in range(TT):
                pool.wait_ge(x_hi, t + 1)
                pool.tensor_tensor(xn[1][:, t], hn[:, t], xn[0][:, t].bitcast(F32), ALU.subtract).then_inc(x_lo, 1)

            def expert(ph, e, fresh=False):
                n = e + E * ph
                for p in range(NP):
                    if not (fresh and p < 2):
                        own(pool, p2_used, NP * n + p - 1)
                    for f in range(FC):
                        own(pool, h_relu, FC * (NP * n + p) + f + 1)
                        pool.tensor_copy(hs[0][:, p % 2, f], hf[:, f]).then_inc(h_hi, 1)

            def experts(ph):
                expert(ph, 0, ph == 0)
                with pool.Fori(1, E) as e:
                    expert(ph, e)

            experts(0)
            overflow(pool, experts)

        @block.scalar
        def _(act):
            def copy(dst, src, signal):
                act.activation(dst, src, ACT.Copy).then_inc(signal, 1)

            def ctx_hi(b, k):
                act.wait_ge(ld_raw[k % 2], 16 * (2 * b + k // 2 + 1))
                copy(cx[0][:, :, k * CC:(k + 1) * CC], raw[:, k % 2], c_hi)

            def root(o):
                act.wait_ge(var_done, o)
                act.activation(stat[:, 44:48], stat[:, 40:44], ACT.Sqrt).then_inc(root_done, 1)

            def key_hi(h, j, bank):
                k, m = j // 2, j % 2
                act.activation(kk[0][:, m, k * KC:(k + 1) * KC], work[bank][:, 0:KC], ACT.Identity,
                               bias=biasT[:, C + 2 * h + m:C + 2 * h + m + 1]).then_inc(kv_hi, 1)

            def kv_item(b, last, step):
                kind, h, j = step
                bank = bank_of(last, step)
                act.wait_ge(w_full, count(b, last, step))
                if kind == "k":
                    key_hi(h, j, bank)
                else:
                    n = min(2, KT - 2 * j)
                    copy(vv[0][:, 2 * j:2 * j + n, :],
                         (ptp if spare(step) else work)[bank][:, 0:n * 2 * P].rearrange("p (n d) -> p n d", n=n), kv_hi)

            def first_keys(js):
                for j in js:
                    act.wait_ge(w_full, j + 1)
                    key_hi(0, j, j % 4)

            act.wait_ge(t_full, 1)
            copy(biasT[:], pv[:, 0:3 * C], t_out)
            def kw_hi(h):
                cols = slice(h * D // 2, (h + 1) * D // 2)
                act.wait_ge(ld_kw[h], 16)
                copy(kw[0][:, :, cols], kwraw[:, :, cols], w_hi)

            kw_hi(0)
            ctx_hi(0, 0)
            ctx_hi(0, 1)
            act.wait_ge(t_out, 1)
            first_keys(range(0, 1))
            root(1)
            first_keys(range(1, 2))
            ctx_hi(0, 2)
            first_keys(range(2, 4))
            for c in range(C):
                act.wait_ge(t_full, c + 2)
                copy(xnT[:, c], yb[c][:], t_out)
            ctx_hi(0, 3)
            kw_hi(1)
            act.wait_ge(ld_vw, 32)
            copy(vw[0][:].rearrange("p (a b) n -> p a b n", a=2), vwraw, w_hi)
            first_keys(range(4, FIRST_K))
            for c in range(C):
                act.wait_ge(t_full, C + 2 + c)
                act.activation(qT[:, c], yb[c][:], ACT.Identity, bias=biasT[:, c:c + 1]).then_inc(q_done, 1)

            def exponentials(b, r):
                act.wait_ge(nmx_done, 8 * b + r + 1)
                row = pr[:, r % 4, 0:LKP]
                act.activation(row, row, ACT.Exp, bias=nmx[:, r:r + 1],
                               accum_out=rsum[:, r:r + 1]).then_inc(exp_done, 1)

            def pt_item(b, j):
                act.wait_ge(pt_full, NPT * b + j + 1)
                act.wait_ge(pt_used, NPT * b + pt_before(j))
                n = min(2, KT - 2 * (j % TPH))
                copy(pt[0][:, j % PTD, 0:n], ptp[j % PTD][:, 0:n * 2 * P].rearrange("p (n d) -> p n d", n=n), pt_hi)

            LAST_READ = {(CC * (k + 1) - 1) // (2 * P): k for k in range(NKC)}

            def body(b, last=False):
                for step in STEPS[last]:
                    kind, a, j = step
                    if kind in "kv":
                        kv_item(b, last, step)
                    if kind == "v" and a == 1 and j in LAST_READ and not last:
                        ctx_hi(b + 1, LAST_READ[j])
                    if kind == "e":
                        exponentials(b, a)
                    for j in turns(step):
                        pt_item(b, j)

            def add_bias(first, end):
                for c in range(C):
                    act.activation(qT[:, c, first:end], qT[:, c, first:end], ACT.Identity,
                                   bias=biasT[:, 2 * C + c:2 * C + c + 1]).then_inc(ob_done, 1)

            with act.Fori(0, LASTB) as b:
                body(b)
            act.wait_ge(pv_free, 4 * LASTB + 1)
            add_bias(0, LASTB * S)
            body(LASTB, True)
            act.wait_ge(pt_hi, NPT * B)
            act.sem_inc(att_over, 1)

            act.wait_ge(att_over, 4)
            add_bias(LASTB * S, T)
            act.wait_ge(m_full, 5)
            copy(b1T[:], pv[:, 0:P], m_out)
            root(2)
            for t in range(TT):
                act.wait_ge(m_full, 6 + t)
                copy(hT[:, :, t * P:(t + 1) * P], yb[t][:].rearrange("p (c n) -> p c n", c=C), m_out)
            def w1_part(ph, e, p, fresh=False):
                s, n = p % 2, e + E * ph
                act.wait_ge(ld_w1[s], 16 * (2 * n + p // 2 + 1))
                if not fresh:
                    act.wait_ge(h_full, HB * (NP * n + p - 1))
                copy(w1s[0][:, s], w1raw[:, s], w1_hi)

            def w2_part(ph, e, p, fresh=False):
                s, n = p % 2, e + E * ph
                act.wait_ge(ld_w2[s], 16 * (2 * n + p // 2 + 1))
                if not fresh:
                    act.wait_ge(p2_used, NP * n + p - 1)
                copy(w2s[0][:, s], w2raw[:, s], w2_hi)

            for p in range(2):
                w1_part(0, 0, p, True)
                w2_part(0, 0, p, True)
            for c in range(C):
                act.wait_ge(m_full, 10 + c)
                copy(gT[:, c], work[c][:], m_out)
            root(3)

            def gathered(n):
                for i in range(2):
                    act.wait_ge(xg_full, 2 * n + i + 1)
                    copy(xg[0][:, 2 * i:2 * i + 2], work[2 + i][:].rearrange("p (c n) -> p c n", c=2), xg_hi)

            def outputs(n):
                act.wait_ge(p2_used, NP * (n + 1))
                if not (isinstance(n, int) and n == 0):
                    act.wait_ge(y_put, TT * n)
                for i in range(ST):
                    copy(ys[0][:, i], yb[i][:], y_hi)

            def expert(ph, e, fresh=False, first=False, last=False):
                n = e + E * ph
                for p in range(NP):
                    if p == NP - 1 and not last:
                        w1_part(ph, e + 1, 0)
                    if p < NP - 1 and not (fresh and p == 0):
                        w1_part(ph, e, p + 1)
                    if not (fresh and p < 2):
                        w2_part(ph, e, p)
                    for f in range(FC):
                        c = FC * (NP * n + p) + f
                        if f % 2 == 0:
                            act.wait_ge(h_full, HB * (NP * n + p) + f // 2 + 1)
                        if not (fresh and p == 0):
                            act.wait_ge(h_lo, c - 3)
                        col = 16 * e + FC * p + f
                        bias = b1T[:, col:col + 1] if isinstance(e, int) else b1T[:, bass.ds(col, 1)]
                        act.activation(hf[:, f], work[f // 2][:, (f % 2) * SLOTS:(f % 2 + 1) * SLOTS],
                                       ACT.Relu, bias=bias).then_inc(h_relu, 1)
                    if p == 0 and not first:
                        outputs(n - 1)
                if not last:
                    gathered(n + 1)

            def experts(ph):
                if ph:
                    w1_part(ph, 0, 0)
                gathered(E * ph)
                expert(ph, 0, ph == 0, first=True)
                with act.Fori(1, LASTE) as e:
                    expert(ph, e)
                expert(ph, LASTE, last=True)
                outputs(E * ph + LASTE)

            for t in range(TT):
                act.wait_ge(ln2, TT + t + 1)
                copy(xn[0][:, t], hn[:, t], x_hi)
                if t % 2:
                    for u in (t - 1, t):
                        act.wait_ge(m_full, 22 + u)
                        copy(hT[:, :, u * P:(u + 1) * P], yb[u][:].rearrange("p (c n) -> p c n", c=C), m_out)
            act.wait_ge(gate_diff, 1)
            act.activation(wts[:, 1], wts[:, 0], ACT.Exp).then_inc(gate_exp, 1)
            experts(0)
            overflow(act, experts)

        @block.tensor
        def _(pe):
            PASSES = ((0, 0), (0, 1), (1, 0))

            def products(dst, lhs, rhs, n=C):
                for c in range(n):
                    for i, j in PASSES:
                        last = pe.matmul(dst, lhs(i, c), rhs(j, c), start=(c == 0 and (i, j) == (0, 0)),
                                         stop=(c == n - 1 and (i, j) == (1, 0)))
                return last

            def plain(dst, lhs, rhs, n=C):
                for c in range(n):
                    last = pe.matmul(dst, lhs(c), rhs(c), start=(c == 0), stop=(c == n - 1))
                return last

            pe.wait_ge(consts, 3)
            pe.wait_ge(ld_b, 16)
            pe.transpose(pv[:, 0:3 * C], brow[:], ident[0:3 * C, 0:3 * C]).then_inc(t_full, 1)

            def key_item(b, h, j, bank):
                k, m = j // 2, j % 2
                if m == 0:
                    pe.wait_ge(c_lo, NKC * b + k + 1)
                products(bank[:, 0:KC], lambda i, c: kw[i][:, c, (2 * h + m) * P:(2 * h + m + 1) * P],
                         lambda i, c: cx[i][:, c, k * KC:(k + 1) * KC]).then_inc(w_full, 1)

            def value_item(h, j, bank):
                for n in range(min(2, KT - 2 * j)):
                    kt = 2 * j + n
                    last = products(bank[:, n * 2 * P:(n + 1) * 2 * P],
                                    lambda i, c: cx[i][:, c, kt * P:(kt + 1) * P],
                                    lambda i, c: vw[i][:, c, h * 2 * P:(h + 1) * 2 * P])
                last.then_inc(w_full, 1)

            def item(b, last, step):
                kind, a, k = step
                bank = (ptp if spare(step) else work)[bank_of(last, step)]
                if not spare(step):
                    pe.wait_ge(w_free, before_bank(b, last, step))
                elif k >= 3 + PTD:
                    pe.wait_ge(w_free, count(b, last, ("v", a, k - PTD)))
                if kind == "k":
                    key_item(b + 1 if a == 0 else b, a, k, bank)
                elif kind == "v":
                    value_item(a, k, bank)
                elif kind == "s":
                    cc, rt = (a % 4) // 2, a % 2
                    if a % 4 == 0 and k == 0:
                        pe.wait_ge(qbd_done, (2 * b + a // 4 + 1) * 2 * HPC)
                    products(bank[:, 0:KC], lambda i_, c: qbd[i_][:, cc, rt, :],
                             lambda i_, c: kk[i_][:, cc, k * KC:(k + 1) * KC], 1).then_inc(w_full, 1)
                else:
                    pe.wait_ge(diag_done, 8 * b + 2 * a + 2)
                    for rt in range(2):
                        last_mm = pe.matmul(bank[:, rt * P:(rt + 1) * P], ones[:],
                                            diag[:, 2 * (a % 2) + rt], start=True, stop=True)
                    last_mm.then_inc(w_full, 1)

            pe.wait_ge(w_lo, 1)
            for j in range(4):
                key_item(0, 0, j, work[j])
            pe.wait_ge(ln1, TT)
            pe.wait_ge(t_out, 1)
            for c in range(C):
                for t in range(TT):
                    last = pe.transpose(yb[c][:, t * P:(t + 1) * P], xin[:, t, c * P:(c + 1) * P], ident[:])
                last.then_inc(t_full, 1)
            for j in range(4, FIRST_K):
                pe.wait_ge(w_free, j - 3)
                key_item(0, 0, j, work[j % 4])
            pe.wait_ge(t_out, C + 1)
            pe.wait_ge(ld_qw, 16)
            for m_ in range(C):
                plain(yb[m_][:], lambda c: qwraw[:, c, m_ * P:(m_ + 1) * P],
                      lambda c: xnT[:, c]).then_inc(t_full, 1)
            pe.wait_ge(w_lo, 3)
            pe.sem_inc(pt_used, PTD)

            def turn(b, last, j):
                g, first = j // TPH, 2 * (j % TPH)
                pe.wait_ge(pt_lo, NPT * b + pt_before(j))
                if j % (2 * TPH) == 0:
                    pe.wait_ge(w_free, count(b, last, ("v", g // 2, TPH - 1)))
                if j % TPH == 0:
                    pe.wait_ge(exp_done, 8 * b + 2 * g + 2)
                for n in range(min(2, KT - first)):
                    for rt in range(2):
                        ins = pe.transpose(ptp[j % PTD][:, (2 * n + rt) * P:(2 * n + rt + 1) * P],
                                            pr[:, (2 * g + rt) % 4, (first + n) * P:(first + n + 1) * P], ident[:])
                ins.then_inc(pt_full, 1)

            def weigh(b, j):
                g, first = j // TPH, 2 * (j % TPH)
                pe.wait_ge(pt_lo, NPT * b + j + 1 + PTD)
                if first == 0:
                    pe.wait_ge(pv_free, 4 * b + g + 1)
                for n in range(min(2, KT - first)):
                    kt = first + n
                    for i, k in PASSES:
                        last = pe.matmul(pv[:, 0:2 * P], vv[i][:, kt, (g % 2) * P:(g % 2 + 1) * P],
                                         pt[k][:, j % PTD, n], start=(kt == 0 and (i, k) == (0, 0)),
                                         stop=(kt == KT - 1 and (i, k) == (1, 0)))
                last.then_inc(pt_used, 1)

            def weighted(b, last, g):
                end = 2 * TPH * (g // 2 + 1)
                for j in range(TPH * g, TPH * (g + 1)):
                    if j + 2 < end:
                        turn(b, last, j + 2)
                    weigh(b, j)

            def body(b, last=False):
                for step in STEPS[last]:
                    if step[0] == "w":
                        weighted(b, last, step[1])
                    elif step[0] == "t":
                        for j in turns(step):
                            turn(b, last, j)
                    elif step[0] in "vskr":
                        item(b, last, step)

            with pe.Fori(0, LASTB) as b:
                body(b)
            body(LASTB, True)
            pe.sem_inc(att_over, 1)

            pe.wait_ge(ob_done, 2 * C)
            for t in range(TT):
                for c in range(C):
                    last = pe.transpose(work[t][:, c * P:(c + 1) * P], qT[:, c, t * P:(t + 1) * P], ident[:])
                last.then_inc(m_full, 1)
            pe.wait_ge(ld2[4], 16)
            pe.transpose(pv[:, 0:P], b1r[:], ident[:]).then_inc(m_full, 1)

            def turn_tiles(k):
                for t in range(TT):
                    pe.wait_ge(ln2, k * TT + t + 1)
                    for c in range(C):
                        last = pe.transpose(yb[t][:, c * P:(c + 1) * P], hn[:, t, c * P:(c + 1) * P], ident[:])
                    last.then_inc(m_full, 1)

            pe.wait_ge(m_out, 1)
            turn_tiles(0)
            pe.wait_ge(m_out, 1 + TT)
            pe.wait_ge(ld2[1], 16)
            for m_ in range(C):
                plain(work[m_][:], lambda c: wq2[:, c, m_ * P:(m_ + 1) * P],
                      lambda c: hT[:, c]).then_inc(m_full, 1)
            pe.wait_ge(m_out, 1 + TT + C)
            for t in range(TT):
                plain(yb[t][:, 0:P], lambda c: hT[:, c, t * P:(t + 1) * P],
                      lambda c: gT[:, c, t * P:(t + 1) * P]).then_inc(m_full, 1)
            for t in range(TT):
                pe.wait_ge(pre_done, 2 * (t + 1))
                pe.matmul(work[t][:], pre[:, t], hn[:, t], start=True, stop=True).then_inc(m_full, 1)
            turn_tiles(1)
            pe.wait_ge(ld2[2], 16)
            for t in range(TT):
                pe.wait_ge(m_out, 1 + TT + C + t + 1)
                last = plain(work[0][:, t * E:(t + 1) * E], lambda c: hT[:, c, t * P:(t + 1) * P],
                             lambda c: gw[:, c])
            last.then_inc(m_full, 1)
            pe.wait_ge(zeroed, 6)
            pe.wait_ge(chosen_done, 1)
            for t in range(TT):
                for u in range(t + 1):
                    last = pe.matmul(work[1][:, t * E:(t + 1) * E], (before if u == t else ones16)[:], chosen[:, u],
                                     start=(u == 0), stop=(u == t))
            last.then_inc(m_full, 1)
            for t in range(TT):
                last = pe.matmul(yb[0][:, 0:E], ones16[:], chosen[:, t],
                                 start=(t == 0), stop=(t == TT - 1))
            last.then_inc(m_full, 1)

            def gather(n):
                pe.wait_ge(pick_done, TT * (n + 1))
                for c in range(C):
                    dst = work[2 + c // 2][:, (c % 2) * SLOTS:(c % 2 + 1) * SLOTS]
                    for t in range(TT):
                        for i in range(2):
                            last = pe.matmul(dst, xn[i][:, t, c * P:(c + 1) * P], pick[:, t],
                                             start=(t == 0 and i == 0), stop=(t == TT - 1 and i == 1))
                    if c % 2:
                        last.then_inc(xg_full, 1)

            def places(n):
                pe.wait_ge(row_done, n + 1)
                pe.wait_ge(y_out, TT * (n + 1))
                pe.matmul(yb[2][:], ones_e[:], place_e[:], start=True, stop=True).then_inc(row_full, 1)

            def scatter(n):
                pe.wait_ge(put_done, ST * (n + 1))
                pe.wait_ge(y_lo, ST * (n + 1))
                for t in range(TT):
                    if t >= 2:
                        pe.wait_ge(y_out, TT * (n + 1) + t - 1)
                    for st in range(ST):
                        for i in range(2):
                            last = pe.matmul(yb[2 + t % 2][:], put[:, st, t * P:(t + 1) * P], ys[i][:, st],
                                             start=(st == 0 and i == 0), stop=(st == ST - 1 and i == 1))
                    last.then_inc(y_put, 1)

            def hidden(n, p, fresh=False):
                s = p % 2
                pe.wait_ge(w1_lo, NP * n + p + 1)
                if p == 0:
                    pe.wait_ge(xg_lo, 2 * (n + 1))
                for f in range(FC):
                    if f % 2 == 0 and not fresh:
                        pe.wait_ge(h_relu, FC * (NP * n + p) + f - 2)
                    last = products(work[f // 2][:, (f % 2) * SLOTS:(f % 2 + 1) * SLOTS],
                             lambda i, c: w1s[i][:, s, c, f * P:(f + 1) * P],
                             lambda i, c: xg[i][:, c])
                    if f % 2:
                        last.then_inc(h_full, 1)

            def second(n, p):
                s = p % 2
                pe.wait_ge(w2_lo, NP * n + p + 1)
                if p == 0:
                    if isinstance(n, int) and n == 0:
                        pe.wait_ge(y_out, TT)
                    else:
                        pe.wait_ge(y_lo, ST * n)
                for f in range(FC):
                    pe.wait_ge(h_lo, FC * (NP * n + p) + f + 1)
                    for st in range(ST):
                        for i, k in PASSES:
                            last = pe.matmul(yb[st][:], hs[i][:, s, f, st * P:(st + 1) * P], w2s[k][:, s, f],
                                             start=(p == 0 and f == 0 and (i, k) == (0, 0)),
                                             stop=(p == NP - 1 and f == FC - 1 and (i, k) == (1, 0)))
                last.then_inc(p2_used, 1)

            def biases():
                pe.wait_ge(cwT_done, 1)
                pe.wait_ge(ld2[5], 16)
                for t in range(TT):
                    pe.matmul(yb[t][:], cwT[:, t * P:(t + 1) * P], b2s[:], start=True, stop=True).then_inc(m_full, 1)

            def turn_rows():
                for t in range(TT):
                    last = pe.transpose(yb[2][0:E, t * P:(t + 1) * P], place[:, t, 0:E], ident[:])
                last.then_inc(m_full, 1)
                pe.wait_ge(cw_done, 1)
                for t in range(TT):
                    last = pe.transpose(yb[3][0:E, t * P:(t + 1) * P], cw[:, t], ident[:])
                last.then_inc(m_full, 1)

            def expert(n, first=False, last=False):
                for p in range(NP):
                    if p == 2 and not last:
                        gather(n + 1)
                    if p == 2:
                        places(n)
                    if p < NP - 1:
                        hidden(n, p + 1)
                    elif not last:
                        hidden(n + 1, 0)
                    if p == 0 and isinstance(n, int) and n == 0:
                        biases()
                    second(n, p)
                    if p == 0 and not first:
                        scatter(n - 1)

            def experts(ph):
                gather(E * ph)
                hidden(E * ph, 0, ph == 0)
                if ph == 0:
                    turn_rows()
                expert(E * ph, first=True)
                with pe.Fori(1, LASTE) as e:
                    expert(e + E * ph)
                expert(E * ph + LASTE, last=True)
                scatter(E * ph + LASTE)

            pe.wait_ge(x_lo, TT)
            experts(0)
            overflow(pe, experts)

        @block.vector
        def _(dve):
            steps = [0]

            def step(ins):
                ins.then_inc(chain, 1)
                steps[0] += 1

            def join():
                dve.wait_ge(chain, steps[0])

            def layer_norm(src, dst, signal, o):
                st = stat[:, 0:24].rearrange("p (t s) -> p t s", t=TT)
                mv = stat[:, 24:32].rearrange("p (t s) -> p t s", t=TT)
                for t in range(TT):
                    step(dve.bn_stats(st[:, t], src[:, t]))
                join()
                for t in range(TT):
                    step(dve.bn_aggr(mv[:, t], st[:, t]))
                join()
                v, root, y, z = (stat[:, c:c + TT] for c in (40, 44, 32, 48))
                dve.tensor_scalar(v, mv[:, :, 1], EPS, None, ALU.add).then_inc(var_done, 1)
                dve.wait_ge(root_done, o)
                for ins in (lambda: dve.reciprocal(y, root),
                            lambda: dve.tensor_tensor(z, y, y, ALU.mult),
                            lambda: dve.tensor_tensor(z, z, v, ALU.mult),
                            lambda: dve.tensor_scalar(z, z, -0.5, 1.5, ALU.mult, ALU.add),
                            lambda: dve.tensor_tensor(y, y, z, ALU.mult)):
                    step(ins())
                    join()
                for t in range(TT):
                    dve.tensor_scalar(dst[:, t], src[:, t], mv[:, t, 0:1], stat[:, 32 + t:33 + t],
                                      ALU.subtract, ALU.mult).then_inc(signal, 1)

            def convert_mask(b):
                dve.wait_ge(ld_mask, 16 * (b + 1))
                dve.tensor_scalar(negmask[:, 0:LK], pr[:, 0, 0:LK].bitcast(I32), 0.0, LOWEST,
                                  ALU.is_gt, ALU.mult).then_inc(mask_done, 1)

            def weight_lo(i, w, whole):
                dve.wait_ge(w_hi, i)
                dve.tensor_tensor(w[1], whole, w[0].bitcast(F32), ALU.subtract).then_inc(w_lo, 1)

            def kw_lo(h):
                cols = slice(h * D // 2, (h + 1) * D // 2)
                weight_lo(h + 1, [w[:, :, cols] for w in kw], kwraw[:, :, cols])

            step(dve.memset(negmask[:, LK:LKP], LOWEST))
            kw_lo(0)
            dve.wait_ge(c_hi, 1)
            dve.tensor_tensor(cx[1][:, :, 0:CC], raw[:, 0], cx[0][:, :, 0:CC].bitcast(F32),
                              ALU.subtract).then_inc(c_lo, 1)
            dve.wait_ge(ld_x, 16)
            layer_norm(xin, xin, ln1, 1)

            def key_lo(h, j, bank):
                k, m = j // 2, j % 2
                sl = slice(k * KC, (k + 1) * KC)
                col = C + 2 * h + m
                dve.scalar_tensor_tensor(out=kk[1][:, m, sl], in0=work[bank][:, 0:KC],
                                         scalar=biasT[:, col:col + 1], in1=kk[0][:, m, sl].bitcast(F32),
                                         op0=ALU.add, op1=ALU.subtract).then_inc(w_free, 1)

            def query_blocks(b, h):
                def parts(a):
                    rows = slice(HD * a, HD * (a + 1))
                    cols = slice((a % 2) * S, (a % 2 + 1) * S)
                    tok = slice(b * S, (b + 1) * S) if isinstance(b, int) else bass.ds(b * S, S)
                    return qT[rows, 2 * h:2 * h + 2, tok], [q[rows, :, a // 2, cols] for q in qbd]

                for a in range(HPC):
                    src, (hi, lo) = parts(a)
                    dve.tensor_copy(hi, src).then_inc(qbd_done, 1)
                own(dve, qbd_done, (2 * b + h) * 2 * HPC + HPC)
                for a in range(HPC):
                    src, (hi, lo) = parts(a)
                    dve.tensor_tensor(lo, src, hi.bitcast(F32), ALU.subtract).then_inc(qbd_done, 1)

            def item(b, last, step):
                kind, a, k = step
                bank = (ptp if spare(step) else work)[bank_of(last, step)]
                if kind in "kv":
                    dve.wait_ge(kv_hi, NKV * b + FIRST_K + KV[last].index(step) + 1)
                if kind == "k":
                    key_lo(a, k, bank_of(last, step))
                elif kind == "v":
                    n = min(2, KT - 2 * k)
                    dve.tensor_tensor(vv[1][:, 2 * k:2 * k + n, :],
                                      bank[:, 0:n * 2 * P].rearrange("p (n d) -> p n d", n=n),
                                      vv[0][:, 2 * k:2 * k + n, :].bitcast(F32), ALU.subtract).then_inc(w_free, 1)
                elif kind == "s":
                    own(dve, w_full, count(b, last, step))
                    sl = slice(k * KC, (k + 1) * KC)
                    dve.tensor_tensor_reduce(pr[:, a % 4, sl], bank[:, 0:KC], negmask[:, sl], SCALE, LOWEST,
                                             ALU.add, ALU.max, smx[:, a, k:k + 1]).then_inc(w_free, 1)
                    if k == NKC - 1:
                        dve.wait_ge(w_free, count(b, last, step))
                        dve.tensor_reduce(nmx[:, a:a + 1], smx[:, a], AX.X, ALU.max,
                                          negate=True).then_inc(raw_nmx, 1)
                        own(dve, raw_nmx, 8 * b + a + 1)
                        dve.tensor_scalar(nmx[:, a:a + 1], nmx[:, a:a + 1], 1024.0, 1 / 1024.0,
                                          ALU.mult, ALU.mult).then_inc(nmx_done, 1)
                else:
                    dve.wait_ge(w_full, count(b, last, step))
                    dve.tensor_copy(recip[:, a % 2], bank[:, 0:2 * P]).then_inc(w_free, 1)

            def reciprocal(b, r):
                dve.wait_ge(exp_done, 8 * b + r + 1)
                dve.reciprocal(rinv[:, r:r + 1], rsum[:, r:r + 1]).then_inc(rinv_done, 1)
                dve.wait_ge(rinv_done, 8 * b + r + 1)
                dve.tensor_scalar(diag[:, r % 4], ident[:], rinv[:, r:r + 1], None, ALU.mult).then_inc(diag_done, 1)

            def pt_item(b, j):
                dve.wait_ge(pt_hi, NPT * b + j + 1)
                n = min(2, KT - 2 * (j % TPH))
                dve.tensor_tensor(pt[1][:, j % PTD, 0:n],
                                  ptp[j % PTD][:, 0:n * 2 * P].rearrange("p (n d) -> p n d", n=n),
                                  pt[0][:, j % PTD, 0:n].bitcast(F32), ALU.subtract).then_inc(pt_lo, 1)

            def group_out(b, last, g):
                dve.wait_ge(pt_used, NPT * b + TPH * (g + 1) + PTD)
                dve.wait_ge(w_free, count(b, last, ("r", g, 0)))
                for a in range(HPC):
                    rows, cols = slice(HD * a, HD * (a + 1)), slice(S * a, S * (a + 1))
                    tok = slice(b * S, (b + 1) * S) if isinstance(b, int) else bass.ds(b * S, S)
                    ins = dve.tensor_tensor(qT[rows, g, tok], pv[rows, cols], recip[rows, g % 2, cols], ALU.mult)
                ins.then_inc(pv_free, 1)

            def body(b, last=False):
                for step in STEPS[last]:
                    kind, a, j = step
                    for i in turns(step):
                        pt_item(b, i)
                    if kind == "w":
                        group_out(b, last, a)
                    if kind == "d":
                        for r in range(2 * a, 2 * a + 4):
                            reciprocal(b, r)
                    if kind in "vskr":
                        item(b, last, step)
                    if step == ("s", 3, NKC - 1):
                        query_blocks(b, 1)
                    if step == ("s", 7, NKC - 1) and not last:
                        query_blocks(b + 1, 0)
                if not last:
                    convert_mask(b + 1)

            for j in range(FIRST_K):
                if j == 4:
                    kw_lo(1)
                    weight_lo(3, [w[:].rearrange("p (a b) n -> p a b n", a=2) for w in vw], vwraw)
                    convert_mask(0)
                dve.wait_ge(kv_hi, j + 1)
                key_lo(0, j, j % 4)
            dve.wait_ge(q_done, C)
            dve.wait_ge(consts, 5)
            query_blocks(0, 0)
            dve.sem_inc(pt_lo, PTD)
            dve.sem_inc(pv_free, 1)
            dve.wait_ge(mask_done, 1)
            with dve.Fori(0, LASTB) as b:
                body(b)
                dve.wait_ge(mask_done, b + 2)
            body(LASTB, True)
            dve.wait_ge(pv_free, 4 * B + 1)
            dve.sem_inc(att_over, 1)

            dve.wait_ge(ld2[0], 16)
            for t in range(TT):
                dve.wait_ge(m_full, t + 1)
                step(dve.tensor_tensor(xs[:, t], xs[:, t], work[t][:], ALU.add))
            join()
            layer_norm(xs, hn, ln2, 2)
            def w1_part(n, p):
                s = p % 2
                dve.wait_ge(w1_hi, NP * n + p + 1)
                dve.tensor_tensor(w1s[1][:, s], w1raw[:, s], w1s[0][:, s].bitcast(F32),
                                  ALU.subtract).then_inc(w1_lo, 1)

            def w2_part(n, p):
                s = p % 2
                dve.wait_ge(w2_hi, NP * n + p + 1)
                dve.tensor_tensor(w2s[1][:, s], w2raw[:, s], w2s[0][:, s].bitcast(F32),
                                  ALU.subtract).then_inc(w2_lo, 1)

            for p in range(2):
                w1_part(0, p)
                w2_part(0, p)
            dve.wait_ge(zeroed, 6)
            for t in range(TT):
                dve.wait_ge(m_full, 14 + t)
                for a in range(2):
                    r = slice(S * a, S * (a + 1))
                    dve.tensor_copy(pre[r, t, r], yb[t][r, r]).then_inc(pre_done, 1)
            for t in range(TT):
                dve.wait_ge(m_full, 18 + t)
                step(dve.tensor_tensor(xs[:, t], xs[:, t], work[t][:], ALU.add))
            join()
            layer_norm(xs, hn, ln2, 3)
            dve.wait_ge(ld2[3], 16)
            dve.wait_ge(m_full, 26)
            dve.tensor_copy(ones_e[:], ones[0:E, :]).then_inc(placeT_done, 1)
            step(dve.tensor_tensor(logit[:], work[0][:, 0:TT * E].rearrange("p (t e) -> p t e", t=TT), gb[:], ALU.add))
            join()
            for t in range(TT):
                step(dve.max(top8[:, t], logit[:, t]))
            join()
            for t in range(TT):
                step(dve.max_index(idx8[:, t], top8[:, t], logit[:, t]))
            dve.tensor_tensor(wts[:, 0], top8[:, :, 1], top8[:, :, 0], ALU.subtract).then_inc(gate_diff, 1)
            join()
            step(dve.tensor_copy(idxf[:], idx8[:]))
            join()
            for k in range(2):
                step(dve.tensor_tensor(best[:, k], iota_e[:], idxf[:, :, k:k + 1].broadcast_to([P, TT, E]),
                                       ALU.is_equal))
            join()
            dve.tensor_tensor(chosen[:], best[:, 0], best[:, 1], ALU.add).then_inc(chosen_done, 1)
            dve.wait_ge(m_full, 27)
            dve.wait_ge(chosen_done, 1)
            dve.scalar_tensor_tensor(out=place[:, :, 0:E], in0=work[1][:, 0:TT * E].rearrange("p (t e) -> p t e", t=TT),
                                     scalar=1.0, in1=chosen[:], op0=ALU.add, op1=ALU.mult).then_inc(place_done, 1)
            dve.wait_ge(place_done, 1)

            def picks(n):
                for t in range(TT):
                    col = place[:, t, n:n + 1] if isinstance(n, int) else place[:, t, bass.ds(n, 1)]
                    dve.tensor_scalar(pick[:, t], iota_s[:], col, None, ALU.is_equal).then_inc(pick_done, 1)

            def gathered(n):
                for i in range(2):
                    dve.wait_ge(xg_hi, 2 * n + i + 1)
                    dve.tensor_tensor(xg[1][:, 2 * i:2 * i + 2], work[2 + i][:].rearrange("p (c n) -> p c n", c=2),
                                      xg[0][:, 2 * i:2 * i + 2].bitcast(F32), ALU.subtract).then_inc(xg_lo, 1)

            def row(n, e):
                mine = ident[0:E, e:e + 1] if isinstance(e, int) else ident[0:E, bass.ds(e, 1)]
                dve.tensor_scalar(place_e[:], placeT[:], mine, None, ALU.mult).then_inc(row_done, 1)

            def puts(ph, n):
                dve.wait_ge(row_full, n + 1)
                for st in range(ST):
                    dve.tensor_scalar(put[:, st], yb[2][:], slot_id[:, ph, st:st + 1], None,
                                      ALU.is_equal).then_inc(put_done, 1)

            def outputs(n):
                for i in range(ST):
                    dve.wait_ge(y_hi, ST * n + i + 1)
                    dve.tensor_tensor(ys[1][:, i], yb[i][:], ys[0][:, i].bitcast(F32), ALU.subtract).then_inc(y_lo, 1)

            def add_outputs(n, e):
                dve.wait_ge(y_out, TT * (n + 1))
                for t in range(TT):
                    dve.wait_ge(y_put, TT * n + t + 1)
                    col = cw[:, t, e:e + 1] if isinstance(e, int) else cw[:, t, bass.ds(e, 1)]
                    dve.scalar_tensor_tensor(out=xs[:, t], in0=yb[2 + t % 2][:], scalar=col, in1=xs[:, t],
                                             op0=ALU.mult, op1=ALU.add).then_inc(y_out, 1)

            def biases():
                for t in range(TT):
                    dve.wait_ge(m_full, 31 + t)
                    dve.tensor_tensor(xs[:, t], xs[:, t], yb[t][:], ALU.add).then_inc(y_out, 1)

            def expert(ph, e, fresh=False, first=False, last=False):
                n = e + E * ph
                for p in range(NP):
                    if p == NP - 1 and not last:
                        w1_part(n + 1, 0)
                    if p < NP - 1 and not (fresh and p == 0):
                        w1_part(n, p + 1)
                    if not (fresh and p < 2):
                        w2_part(n, p)
                    for f in range(FC):
                        c = FC * (NP * n + p) + f
                        dve.wait_ge(h_hi, c + 1)
                        dve.tensor_tensor(hs[1][:, p % 2, f], hf[:, f], hs[0][:, p % 2, f].bitcast(F32),
                                          ALU.subtract).then_inc(h_lo, 1)
                    if p == 0 and not first:
                        outputs(n - 1)
                    if p == 0 and isinstance(n, int) and n == 0:
                        biases()
                    if p == 1:
                        if not first:
                            add_outputs(n - 1, e - 1)
                        row(n, e)
                        if not last:
                            picks(n + 1)
                    if p == 2:
                        puts(ph, n)
                if not last:
                    gathered(n + 1)

            def experts(ph):
                if ph:
                    w1_part(E * ph, 0)
                    picks(E * ph)
                    gathered(E * ph)
                expert(ph, 0, ph == 0, first=True)
                with dve.Fori(1, LASTE) as e:
                    expert(ph, e)
                expert(ph, LASTE, last=True)
                outputs(E * ph + LASTE)
                add_outputs(E * ph + LASTE, LASTE)
                dve.wait_ge(y_out, TT * (E * (ph + 1) + 1))

            picks(0)
            dve.wait_ge(gate_exp, 1)
            step(dve.tensor_scalar(wts[:, 0], wts[:, 1], 1.0, None, ALU.add))
            step(dve.tensor_scalar(place[:, :, E:2 * E], place[:, :, 0:E], -float(SLOTS), None, ALU.add))
            join()
            step(dve.reciprocal(wts[:, 2], wts[:, 0]))
            join()
            step(dve.tensor_tensor(wts[:, 3], wts[:, 1], wts[:, 2], ALU.mult))
            gathered(0)
            dve.wait_ge(m_full, 28)
            step(dve.tensor_reduce(total[:, 0:1], yb[0][:, 0:E], AX.X, ALU.max))
            join()
            for k, dst in ((0, cw), (1, cw2)):
                step(dve.tensor_tensor(dst[:], best[:, k], wts[:, 2 + k].rearrange("p (t o) -> p t o", o=1)
                                       .broadcast_to([P, TT, E]), ALU.mult))
            join()
            dve.tensor_tensor(cw[:], cw[:], cw2[:], ALU.add).then_inc(cw_done, 1)
            dve.tensor_scalar(crowded[:], total[:, 0:1], float(SLOTS), None, ALU.is_gt).then_inc(flag_done, 1)
            dve.wait_ge(m_full, 29)
            step(dve.tensor_copy(placeT[:], yb[2][0:E, :]))
            dve.wait_ge(m_full, 30)
            dve.tensor_copy(cwT[:], yb[3][0:E, :]).then_inc(cwT_done, 1)
            join()
            experts(0)
            overflow(dve, experts)
            dve.sem_inc(result_done, 1)


def kernel(**inputs):
    import numpy as np
    import concourse.bacc as bacc
    from concourse.bass_utils import run_bass_kernel_spmd

    def a(name):
        return np.asarray(inputs[name])

    ctxT = np.zeros((B, D, KP), np.float32)
    ctxT[:, :, :LK] = a("ctx_1024").transpose(0, 2, 1)
    arrays = {
        "x": a("x").reshape(T, D), "ctxT": ctxT, "mask": a("mask_BxS2_ik0"),
        "qwT": a("L0_xattn_q_w").T, "kwT": a("L0_xattn_k_w").T, "vwT": a("L0_xattn_v_w").T,
        "wqT": a("L0_attn_W_q").T,
        "bias3": np.concatenate([a("L0_xattn_q_b"), a("L0_xattn_k_b"), a("L0_xattn_v_b")]).reshape(3 * C, P),
        "gate_w": a("L0_ffn_gate_w"), "gate_b": np.tile(a("L0_ffn_gate_b"), TT).reshape(1, TT * E),
        "w1": a("L0_ffn_w1"), "b1": a("L0_ffn_b1"), "w2": a("L0_ffn_w2"), "b2": a("L0_ffn_b2"),
    }
    arrays = {f"in_{n}": np.ascontiguousarray(v) for n, v in arrays.items()}
    nc = bacc.Bacc("TRN2", target_bir_lowering=False, num_devices=1)
    args = [nc.dram_tensor(n, v.shape, mybir.dt.from_np(v.dtype), kind="ExternalInput").ap()
            for n, v in arrays.items()]
    out = nc.dram_tensor("out", (T, D), F32, kind="ExternalOutput").ap()
    layer(nc, *args, out)
    r = run_bass_kernel_spmd(nc, [arrays], core_ids=[0])
    return r.results[0]["out"].reshape(B, S, D)
```
